# Optimizing a Trainium2 kernel written in Bass

```python
import numpy as np
import jax
import jax.numpy as jnp

def _softmax(x, axis=-1):
    return jax.nn.softmax(x, axis=axis)

def _gelu(x):
    return jax.nn.gelu(x, approximate=True)

def _silu(x):
    return jax.nn.silu(x)

def _sigmoid(x):
    return jax.nn.sigmoid(x)

def _layernorm(x, axis=-1, eps=1e-05):
    m = jnp.mean(x, axis=axis, keepdims=True)
    v = jnp.var(x, axis=axis, keepdims=True)
    return (x - m) / jnp.sqrt(v + eps)

def _scatter_add(tgt, idx, src, axis=0):
    return tgt.at[idx].add(src)

def _segment_sum(src, seg, n):
    return jax.ops.segment_sum(src, seg, n)
kernel_name = 'mk_adj_ffn_d1_adj_r2_b4f3a0'

def setup_inputs(seed: int=0):
    np.random.seed(seed)
    _w = jnp.asarray

    def _rec_inputs():
        import jax
        import jax.numpy as jnp
        _gk = jax.random.key(seed)
        x = -0.0002928 + 1 * jax.random.normal(jax.random.fold_in(_gk, 1), (3327, 256), jnp.float32)
        _a = jax.random.bernoulli(jax.random.fold_in(_gk, 2), 0.00480914, (3327, 3327))
        _af = _a.astype(jnp.float32)
        adj = _af
        return (x, adj)
    x, adj = _rec_inputs()

    def _L0_gnn_setup():
        import jax, jax.numpy as jnp
        import numpy as np
        N = 4096
        D_IN = 256
        HEADS = 8
        DPH = 256 // HEADS
        EDGE_P = 0.01
        key = jax.random.key(seed)
        k1, k2, k3 = jax.random.split(key, 3)
        H = jax.random.normal(k1, (N, D_IN), dtype=jnp.float32)
        adj = (jax.random.uniform(k2, (N, N)) < EDGE_P).astype(jnp.float32)
        limit = float(np.sqrt(6.0 / (D_IN + DPH)))
        W = jax.random.uniform(k3, (HEADS, D_IN, DPH), jnp.float32, -limit, limit)
        b = jnp.zeros((HEADS, DPH), jnp.float32)
        return {'H': H, 'adj': adj, 'W': W, 'b': b}
    _L0_gnn_all = _L0_gnn_setup()
    _L0_gnn_in = {k: v for k, v in _L0_gnn_all.items() if k in ('W', 'b')}
    del _L0_gnn_all

    def _L0_ffn_setup():
        import jax, jax.numpy as jnp
        import numpy as np
        B, S, D, H, E = (4, 512, 256, 1024, 8)
        key = jax.random.key(seed)
        ks = jax.random.split(key, 7)
        scale = 1.0 / np.sqrt(D)
        return {'x': jax.random.normal(ks[0], (B, S, D), dtype=jnp.float32), 'Wg': jax.random.normal(ks[1], (D, E), dtype=jnp.float32) * scale, 'bg': jnp.zeros((E,), dtype=jnp.float32), 'W1': jax.random.normal(ks[2], (E, D, H), dtype=jnp.float32) * scale, 'b1': jnp.zeros((E, H), dtype=jnp.float32), 'W2': jax.random.normal(ks[3], (E, H, D), dtype=jnp.float32) * (1.0 / np.sqrt(H)), 'b2': jnp.zeros((E, D), dtype=jnp.float32)}
    _L0_ffn_all = _L0_ffn_setup()
    _L0_ffn_in = {k: v for k, v in _L0_ffn_all.items() if k in ('Wg', 'bg', 'W1', 'b1', 'W2', 'b2')}
    del _L0_ffn_all
    return {'x': x, 'adj': adj, 'L0_gnn_W': _L0_gnn_in['W'], 'L0_gnn_b': _L0_gnn_in['b'], 'L0_ffn_Wg': _L0_ffn_in['Wg'], 'L0_ffn_bg': _L0_ffn_in['bg'], 'L0_ffn_W1': _L0_ffn_in['W1'], 'L0_ffn_b1': _L0_ffn_in['b1'], 'L0_ffn_W2': _L0_ffn_in['W2'], 'L0_ffn_b2': _L0_ffn_in['b2']}

def reference(x, adj, L0_gnn_W, L0_gnn_b, L0_ffn_Wg, L0_ffn_bg, L0_ffn_W1, L0_ffn_b1, L0_ffn_W2, L0_ffn_b2):
    import jax
    import jax.numpy as jnp

    def _L0_gnn_ref(H, adj, W, b):
        import jax, jax.numpy as jnp
        import numpy as np
        N = 4096
        D_IN = 256
        HEADS = 8
        DPH = 256 // HEADS
        EDGE_P = 0.01
        H_ = jnp.einsum('nd,hde->hne', H, W)
        out = jnp.einsum('nm,hme->hne', adj, H_) + b[:, None, :]
        return jnp.transpose(out, (1, 0, 2)).reshape(H.shape[0], HEADS * DPH)

    def _L0_ffn_ref(x, Wg, bg, W1, b1, W2, b2):
        import jax, jax.numpy as jnp
        import numpy as np
        B, S, D, H, E = (4, 512, 256, 1024, 8)
        b, s, d = x.shape
        xf = x.reshape(-1, d)
        logits = xf @ Wg + bg
        scores = jax.nn.softmax(logits, axis=-1)
        top_s, top_i = jax.lax.top_k(scores, 1)
        idx = top_i[:, 0]
        sc = top_s[:, 0]
        n_experts = Wg.shape[1]
        out = jnp.zeros_like(xf)
        for e in range(n_experts):
            h = jax.nn.relu(xf @ W1[e] + b1[e]) @ W2[e] + b2[e]
            out = jnp.where((idx == e)[:, None], h, out)
        out = out * sc[:, None]
        return out.reshape(b, s, d)
    x = x + _L0_gnn_ref(_layernorm(x, axis=-1), adj, L0_gnn_W, L0_gnn_b)
    x = x + _L0_ffn_ref(_layernorm(x, axis=-1)[None], L0_ffn_Wg, L0_ffn_bg, L0_ffn_W1, L0_ffn_b1, L0_ffn_W2, L0_ffn_b2)[0]
    return x

_drawn_inputs = setup_inputs


def setup_inputs(seed=0):
    import zlib

    import numpy as np

    out = dict(_drawn_inputs(seed))
    spreads = {'L0_gnn_b': (0.0, 0.403),
     'L0_ffn_bg': (0.0, 0.721),
     'L0_ffn_b1': (0.0, 0.8),
     'L0_ffn_b2': (0.0, 0.8)}
    factors = {}
    for name, (base, spread) in spreads.items():
        noise = np.random.default_rng([zlib.crc32(name.encode()), seed]).standard_normal(out[name].shape)
        drawn = base * np.exp(spread * noise) if base else spread * noise
        out[name] = jnp.asarray(drawn.astype(out[name].dtype))
    for name, factor in factors.items():
        out[name] = (out[name] * factor).astype(out[name].dtype)
    return out
```

```python
from contextlib import ExitStack

import concourse.bass as bass
from concourse import mybir

ALU = mybir.AluOpType
ACT = mybir.ActivationFunctionType
AX = mybir.AxisListType
F32 = mybir.dt.float32
F16 = mybir.dt.float16
BF16 = mybir.dt.bfloat16
U16 = mybir.dt.uint16
I32 = mybir.dt.int32

P = 128
N = 3327
D = 256
DK = D // P
TILES = -(-N // P)
NPAD = TILES * P
CT = 2
CHUNKS = TILES // CT
CHUNK_WORDS = TILES * CT * P
E = 8
HID = 1024
HB = HID // P
SLOT_TILES = (N + E * (P - 1)) // P
ROW = D + 4
EPS = 1e-5
ADJ_BUFS = 3
GNN_UNROLL = 2 * ADJ_BUFS
FFN_RING = 3
EXPERT_WORDS = DK * HID + HB * D
EARLY = 1
ACT_PART = 2560
SKIP = 100000.0
SCALE_EXP = 201
INV_EXP = 254 - SCALE_EXP

assert (CHUNKS - 1) % GNN_UNROLL == 0 and SLOT_TILES % FFN_RING == 0


class Chain:

    def __init__(self, eng, sem):
        self.eng, self.sem, self.base, self.n = eng, sem, 0, 0

    def enter(self, base):
        self.base, self.n = base, 0

    def mark(self, ins):
        self.n += 1
        ins.then_inc(self.sem, 1)

    def wait(self):
        self.eng.wait_ge(self.sem, self.base + self.n)

    def step(self, ins):
        self.mark(ins)
        self.wait()


def build(nc, x, adj, w_gnn, b_gnn, w_gate, b_gate, w_exp, b1, b2, out):
    with ExitStack() as ctx:
        def sb(name, shape, dt=F32):
            return ctx.enter_context(nc.sbuf_tensor(name, shape, dt))

        def ps(name, shape):
            return ctx.enter_context(nc.psum_tensor(name, shape, F32))

        def sem(name):
            return ctx.enter_context(nc.semaphore(name))

        x2_rows = nc.dram_tensor("x2_rows", (NPAD, ROW), F32, kind="Internal").ap()

        ADJ0 = EARLY * EXPERT_WORDS
        HP0 = ADJ0 + ADJ_BUFS * CHUNK_WORDS
        arena = sb("arena", [P, max(HP0 + TILES * D + ACT_PART // 2, E * EXPERT_WORDS)])
        adj_sb = [arena[:, ADJ0 + s * CHUNK_WORDS:ADJ0 + (s + 1) * CHUNK_WORDS] for s in range(ADJ_BUFS)]
        adj_f32 = [a.rearrange("p (k n) -> p k n", n=CT * P) for a in adj_sb]
        adj_half = [a.bitcast(BF16).rearrange("p (k n two) -> p k n two", n=CT * P, two=2) for a in adj_sb]
        adj_bits = [a.bitcast(U16).rearrange("p (w two) -> p w two", two=2) for a in adj_sb]
        junk = arena[:, HP0 + TILES * D:HP0 + TILES * D + ACT_PART // 2].bitcast(BF16)
        h_parts = arena[:, HP0:HP0 + TILES * D].bitcast(F16).rearrange("p (k s d) -> p k s d", s=2, d=D)
        x_sb = sb("x_sb", [P, TILES, D])
        reuse = sb("reuse", [P, TILES * D])
        h_full = reuse[:, :].rearrange("p (k d) -> p k d", d=D)

        ident = sb("ident", [P, P])
        ones = sb("ones", [P, P])
        zeros = sb("zeros", [P, D])
        earlier = sb("earlier", [P, P])
        w_sb = sb("w_sb", [P, DK, D])
        wg_sb = sb("wg_sb", [P, DK, E])
        bg_sb = sb("bg_sb", [P, CT, E])
        b1_sb = sb("b1_sb", [P, E, HB])
        b_bc = sb("b_bc", [P, D])
        inv_scale = sb("inv_scale", [P, D])
        stats = sb("stats", [P, TILES, 6])
        mv = sb("mv", [P, TILES, 2])
        rstd = sb("rstd", [P, TILES])
        nmr = sb("nmr", [P, TILES])
        xn = sb("xn", [P, 2, CT, D])
        xnT = sb("xnT", [P, 2, CT, DK, P])
        rows = sb("rows", [P, 2, CT, ROW])
        lo_sum = sb("lo_sum", [P, CT, D])
        stats2 = sb("stats2", [P, CT, 6])
        mv2 = sb("mv2", [P, CT, 2])
        std2 = sb("std2", [P, CT])
        logits = sb("logits", [P, TILES, E])
        low_any = sb("low_any", [P, 2, 2])
        low_top = sb("low_top", [1, 1])
        redo = sb("redo", [1, 1], I32)

        iota_tile = sb("iota_tile", [P, SLOT_TILES])
        iota_slot = sb("iota_slot", [P, P])
        token_no = sb("token_no", [P, TILES])
        padding = sb("padding", [P, TILES])
        is_token = sb("is_token", [P, TILES])
        down = sb("down", [P, E])
        slot_row = sb("slot_row", [P, SLOT_TILES], I32)
        slot_score = sb("slot_score", [P, SLOT_TILES])
        expert_no = sb("expert_no", [1, SLOT_TILES], I32)
        row_in = sb("row_in", [P, FFN_RING], I32)
        row_out = sb("row_out", [P, FFN_RING], I32)
        score_now = sb("score_now", [P, FFN_RING])
        b1_now = sb("b1_now", [P, FFN_RING, HB])

        class Cut:
            def __init__(self, ap, size):
                self.ap, self.at, self.size = ap, 0, size

            def take(self, n):
                self.at += n
                assert self.at <= self.size
                return self.ap[:, self.at - n:self.at]

        cut = Cut(x_sb[:, :, :].rearrange("p k d -> p (k d)"), TILES * D)
        slot_mask = cut.take(TILES * P).rearrange("p (k s) -> p k s", s=P)
        tile_mask = cut.take(TILES * 2 * SLOT_TILES).rearrange("p (k w) -> p k w", w=2 * SLOT_TILES)
        soft = cut.take(TILES * E).rearrange("p (k e) -> p k e", e=E)
        pick = cut.take(TILES * E).rearrange("p (k e) -> p k e", e=E)
        onehot_f = cut.take(E * TILES)
        onehot = onehot_f.rearrange("p (e k) -> p e k", e=E)
        slot_no = cut.take(E * TILES).rearrange("p (e k) -> p e k", e=E)
        ones_w = cut.take(E * TILES)
        top = cut.take(TILES)
        first = cut.take(TILES)
        score = cut.take(TILES)
        running = cut.take(1 + E * TILES)
        tiles_i = cut.take(E).bitcast(I32)
        tiles_f = cut.take(E)
        tile_end = cut.take(E)
        start_e = cut.take(E)
        pos = cut.take(TILES)
        pos_i = cut.take(3 * TILES).bitcast(I32).rearrange("p (w k) -> p w k", w=3)
        pos_f = cut.take(2 * TILES).rearrange("p (w k) -> p w k", w=2)
        cut = Cut(xnT[:, :, :, :, :].rearrange("p s c k t -> p (s c k t)"), 2 * CT * D)
        ended = cut.take(SLOT_TILES * E)[0:1, :].rearrange("p (i e) -> p i e", e=E)
        expert_f = cut.take(SLOT_TILES)[0:1, :]
        row_f = cut.take(SLOT_TILES)

        cut2 = Cut(reuse, TILES * D)
        b2_sb = cut2.take(E * D).rearrange("p (e d) -> p e d", d=D)
        h_sb = cut2.take(HID)
        hT_sb = cut2.take(HID).rearrange("p (j t) -> p j t", t=P)
        got = [cut2.take(ROW) for _ in range(FFN_RING)]
        done = [cut2.take(D) for _ in range(FFN_RING)]
        fx = cut2.take(D)
        fxT = cut2.take(D).rearrange("p (k t) -> p k t", t=P)
        yb = cut2.take(D)

        p_agg = [ps(f"p_agg{s}", [P, CT, 512]) for s in range(2)]
        p_T = [ps(f"p_T{s}", [P, CT, DK, P]) for s in range(2)]
        p_S = ps("p_S", [P, 512])
        p_y = ps("p_y", [P, 512])
        p_log = [p_y[:, s * 64:s * 64 + CT * E].rearrange("p (c e) -> p c e", e=E) for s in range(2)]
        p_h = p_agg[0][:, :, :].rearrange("p c n -> p (c n)")
        p_hT = p_agg[1][:, :, :].rearrange("p c (j t) -> p (c j) t", t=P)
        p_xT = p_T[0][:, 0, :, :]
        p_rank, p_count = (t[:, :, :, :].rearrange("p c k t -> p (c k t)")[:, 0:E * TILES] for t in p_T)

        s_x = [sem(f"x_loaded{i}") for i in range(2)]
        s_wg = sem("w_gnn_loaded")
        s_small = sem("small_loaded")
        s_adj = [sem(f"adj_loaded{i}") for i in range(ADJ_BUFS)]
        s_w = [sem(f"weights_loaded{i}") for i in range(2)]
        s_const = sem("constants_made")
        s_pool = sem("pool_chain")
        s_dve = sem("dve_chain")
        s_wsq = sem("w_squared")
        s_norm = sem("column_norms_summed")
        s_wscaled = sem("w_scaled")
        s_var = sem("variances_ready")
        s_std = sem("stds_ready")
        s_xn = sem("xn_ready")
        s_T = sem("xn_transposed")
        s_Ts = sem("xnT_in_sbuf")
        s_H = sem("h_summed")
        s_hi = sem("h_high_and_full_copied")
        s_lo = sem("h_low_copied")
        s_xb = sem("b_added_to_x")
        s_chkv = sem("low_halves_checked_dve")
        s_chka = sem("low_halves_checked_act")
        s_flag = sem("flags_summed")
        s_lowtop = sem("flags_reduced")
        s_redo = sem("redo_known")
        s_agg = sem("chunk_aggregated")
        s_losum = sem("low_sum_copied")
        s_free = sem("aggregate_read")
        s_var2 = sem("var2_ready")
        s_std2 = sem("std2_ready")
        s_xn2 = sem("xn2_ready")
        s_row = sem("rows_ready")
        s_stored = sem("rows_stored")
        s_rowfree = sem("row_slot_free")
        s_T2 = sem("xn2_transposed")
        s_T2s = sem("xn2T_in_sbuf")
        s_log = sem("logits_summed")
        s_logs = sem("logits_in_sbuf")
        s_soft = sem("softmax_argument_ready")
        s_exp = sem("exp_ready")
        s_onehot = sem("onehot_ready")
        s_rank = sem("ranks_summed")
        s_masks = sem("masks_ready")
        s_slots = sem("slots_summed")
        s_table = sem("tables_ready")
        s_clear = sem("gather_buffers_cleared")
        s_got = [sem(f"rows_gathered{i}") for i in range(FFN_RING)]
        s_now = sem("tile_columns_copied")
        s_fx = sem("ffn_xn_ready")
        s_fT = sem("ffn_xn_transposed")
        s_fTs = sem("ffn_xnT_in_sbuf")
        s_h = sem("hidden_summed")
        s_hsa = sem("hidden_copied_act")
        s_hsv = sem("hidden_copied_dve")
        s_hT = sem("hidden_transposed")
        s_hTa = sem("hiddenT_relu_act")
        s_hTv = sem("hiddenT_relu_dve")
        s_y = sem("ffn_summed")
        s_yb = sem("ffn_sum_read")
        s_done = sem("rows_finished")
        s_out = [sem(f"rows_scattered{i}") for i in range(FFN_RING)]
        SMALL = 16 * 4

        block = ctx.enter_context(nc.Block())

        @block.sync
        def _(sp):
            sp.dma_start(w_sb[:, :, :], w_gnn).then_inc(s_wg, 16)
            half = TILES // 2
            for i in range(2):
                sp.dma_start(x_sb[:, i * half:(i + 1) * half, :], x[:, i * half:(i + 1) * half, :]).then_inc(s_x[i], 16)
            for c in range(ADJ_BUFS):
                sp.dma_start(adj_sb[c], adj[c]).then_inc(s_adj[c], 16)

            def load_expert(e):
                if e >= 1:
                    sp.wait_ge(s_w[e % 2], 16 * ((e + 1) // 2))
                sp.dma_start(arena[:, e * EXPERT_WORDS:(e + 1) * EXPERT_WORDS], w_exp[e]).then_inc(s_w[e % 2], 16)

            def reload(c, buf):
                sp.wait_ge(s_agg, c - (ADJ_BUFS - 1))
                sp.dma_start(adj_sb[buf], adj[bass.ds(c, 1), :, :].rearrange("c p w -> p (c w)")).then_inc(s_adj[buf], 16)

            turns = (CHUNKS - ADJ_BUFS) // ADJ_BUFS
            with sp.Fori(0, turns) as r:
                for u in range(ADJ_BUFS):
                    reload(r * ADJ_BUFS + (ADJ_BUFS + u), u)
            for c in range(ADJ_BUFS + turns * ADJ_BUFS, CHUNKS):
                reload(c, c % ADJ_BUFS)
            for e in range(EARLY):
                load_expert(e)
            sp.wait_ge(s_agg, CHUNKS)
            sp.dma_start(b2_sb.rearrange("p e d -> p (e d)"), b2.to_broadcast([P, E * D])).then_inc(s_w[1], 16)
            for e in range(EARLY, E):
                load_expert(e)

        @block.gpsimd
        def _(pool):
            pool.dma_start(wg_sb[:, :, :], w_gate).then_inc(s_small, 16)
            pool.dma_start(bg_sb[:, :, :], b_gate.unsqueeze(0).to_broadcast([P, CT, E])).then_inc(s_small, 16)
            pool.dma_start(b1_sb[:, :, :], b1).then_inc(s_small, 16)
            pool.dma_start(b_bc[:, :], b_gnn.to_broadcast([P, D])).then_inc(s_small, 16)
            chain = Chain(pool, s_pool)
            chain.mark(pool.memset(ones[:, :], 1.0))
            chain.mark(pool.memset(ident[:, :], 0.0))
            chain.mark(pool.memset(zeros[:, :], 0.0))
            chain.mark(pool.memset(padding[:, :], 0.0))
            chain.mark(pool.memset(rows[:, :, :, D:ROW], 0.0))
            chain.wait()
            pool.affine_select(out=ident[:, :], in_=ident[:, :], compare_op=ALU.not_equal, fill=1.0,
                               base=0, pattern=[[-1, P]], channel_multiplier=1).then_inc(s_const, 1)
            pool.affine_select(out=earlier[:, :], in_=ones[:, :], compare_op=ALU.is_gt, fill=0.0,
                               base=0, pattern=[[1, P]], channel_multiplier=-1).then_inc(s_const, 1)
            pool.affine_select(out=padding[:, :], in_=padding[:, :], compare_op=ALU.is_gt, fill=1.0,
                               base=N, pattern=[[-P, TILES]], channel_multiplier=-1).then_inc(s_const, 1)
            for table, pattern, base, step in ((iota_tile, [[1, SLOT_TILES]], 0, 0), (iota_slot, [[1, P]], 0, 0),
                                               (token_no, [[P, TILES]], 1, 1), (down, [[-1, E]], E, 0)):
                pool.iota(table[:, :], pattern, base=base, channel_multiplier=step,
                          allow_small_or_imprecise_dtypes=True).then_inc(s_const, 1)

            pool.wait_ge(s_small, SMALL)
            for t in range(CHUNKS):
                pool.wait_ge(s_xn, t + 1)
                for j in range(CT):
                    k = t * CT + j
                    pool.tensor_tensor(x_sb[:, k, :], x_sb[:, k, :], b_bc[:, :], ALU.add).then_inc(s_xb, 1)

            pool.sem_inc(s_rowfree, 2)
            for c in range(CHUNKS):
                pool.wait_ge(s_row, c + 1)
                pool.dma_start(x2_rows[c * CT * P:(c + 1) * CT * P, :].rearrange("(t p) r -> p t r", p=P),
                               rows[:, c % 2, :, :]).then_inc(s_stored, 16)
                pool.wait_ge(s_stored, 16 * (c + 1))
                pool.sem_inc(s_rowfree, 1)

            pool.wait_ge(s_agg, CHUNKS)
            for g in got:
                pool.memset(g, 0.0).then_inc(s_clear, 1)
            pool.wait_ge(s_clear, FFN_RING)
            pool.wait_ge(s_table, 1)

            def gather(i, slot, expert):
                pool.tensor_copy(row_in[:, slot:slot + 1], slot_row[:, bass.ds(i, 1)]).then_inc(s_now, 1)
                pool.tensor_copy(score_now[:, slot:slot + 1], slot_score[:, bass.ds(i, 1)]).then_inc(s_now, 1)
                pool.tensor_copy(b1_now[:, slot, :], b1_sb[:, bass.ds(expert, 1), :].rearrange("p e j -> p (e j)")).then_inc(s_now, 1)
                pool.wait_ge(s_now, 3 * i + 3)
                pool.nop(nofuse=True)
                pool.indirect_dma_start(got[slot], None, x2_rows,
                                        bass.IndirectOffsetOnAxis(ap=row_in[:, slot:slot + 1], axis=0),
                                        bounds_check=N - 1, oob_is_err=False).then_inc(s_got[slot], 16)

            def scatter(i, k, slot):
                if not isinstance(k, int) or k >= 1:
                    pool.wait_ge(s_out[slot], 16 * k)
                pool.tensor_copy(row_out[:, slot:slot + 1], slot_row[:, bass.ds(i, 1)]).then_inc(s_pool, 1)
                pool.wait_ge(s_pool, 5 + i + 1)
                pool.wait_ge(s_done, i + 1)
                pool.nop(nofuse=True)
                pool.indirect_dma_start(out, bass.IndirectOffsetOnAxis(ap=row_out[:, slot:slot + 1], axis=0),
                                        done[slot], None, bounds_check=N - 1, oob_is_err=False).then_inc(s_out[slot], 16)

            def expert_of(i):
                return pool.value_load(expert_no[0:1, bass.ds(i, 1)], min_val=0, max_val=E - 1)

            for i in range(FFN_RING):
                gather(i, i, expert_of(i))
            for i in range(FFN_RING):
                scatter(i, 0, i)
                gather(i + FFN_RING, i, expert_of(i + FFN_RING))
            with pool.Fori(1, SLOT_TILES // FFN_RING - 1) as k:
                for u in range(FFN_RING):
                    i = k * FFN_RING + u
                    scatter(i, k, u)
                    gather(i + FFN_RING, u, expert_of(i + FFN_RING))
            for i in range(SLOT_TILES - FFN_RING, SLOT_TILES):
                scatter(i, i // FFN_RING, i % FFN_RING)
            for slot in range(FFN_RING):
                pool.wait_ge(s_out[slot], 16 * (SLOT_TILES // FFN_RING))

        @block.scalar
        def _(act):
            act.wait_ge(s_var, 1)
            nc.scalar.activation(rstd[:, :], rstd[:, :], ACT.Sqrt).then_inc(s_std, 1)

            def copy_xnT(t, slot, transposed, copied):
                act.wait_ge(transposed, t + 1)
                nc.scalar.activation(xnT[:, slot, :, :, :], p_T[slot][:, :, :, :], ACT.Copy).then_inc(copied, 1)

            def keep_h(t, slot):
                act.wait_ge(s_H, t + 1)
                nc.scalar.activation(h_parts[:, bass.ds(t * CT, CT), 0, :], p_agg[slot][:, :, 0:D], ACT.Copy).then_inc(s_hi, 1)
                nc.scalar.activation(h_full[:, bass.ds(t * CT, CT), :], p_agg[slot][:, :, 0:D], ACT.Copy).then_inc(s_hi, 1)

            copy_xnT(0, 0, s_T, s_Ts)
            with act.Fori(0, (CHUNKS - 1) // 2) as r:
                for u in range(2):
                    copy_xnT(r * 2 + (u + 1), 1 - u, s_T, s_Ts)
                    keep_h(r * 2 + u, u)
            keep_h(CHUNKS - 1, 0)

            def check(c, k, buf, slot):
                act.wait_ge(s_adj[buf], 16 * k)
                nc.scalar.activation(junk, adj_bits[buf][:, 0:ACT_PART, 0], ACT.Copy,
                                     accum_out=low_any[:, slot, 0:1]).then_inc(s_chka, 1)

            def low_sum(c, slot):
                act.wait_ge(s_agg, c + 1)
                act.wait_ge(s_free, c + 2)
                nc.scalar.activation(lo_sum[:, :, :], p_agg[slot][:, :, D:2 * D], ACT.Copy).then_inc(s_losum, 1)

            def std(c):
                act.wait_ge(s_var2, c + 1)
                nc.scalar.activation(std2[:, :], mv2[:, :, 1], ACT.Sqrt).then_inc(s_std2, 1)

            check(0, 1, 0, 0)
            low_sum(0, 0)
            with act.Fori(0, (CHUNKS - 1) // GNN_UNROLL) as r:
                for u in range(GNN_UNROLL):
                    c = r * GNN_UNROLL + (u + 1)
                    check(c, r * 2 + ((u + 1) // ADJ_BUFS + 1), (u + 1) % ADJ_BUFS, (u + 1) % 2)
                    std(c - 1)
                    copy_xnT(c - 1, u % 2, s_T2, s_T2s)
                    low_sum(c, (u + 1) % 2)
            std(CHUNKS - 1)
            copy_xnT(CHUNKS - 1, (CHUNKS - 1) % 2, s_T2, s_T2s)

            act.wait_ge(s_soft, 1)
            nc.scalar.activation(soft, soft, ACT.Exp).then_inc(s_exp, 1)

            HALF = HID // 2

            def relu_hT(i, slot):
                act.wait_ge(s_hT, i + 1)
                if not isinstance(i, int) or i >= 1:
                    act.wait_ge(s_y, i)
                act.wait_ge(s_now, 3 * i + 3)
                for j in range(HB // 2):
                    last = nc.scalar.activation(hT_sb[:, j, :], p_hT[:, j, :], ACT.Relu, bias=b1_now[:, slot, j:j + 1])
                last.then_inc(s_hTa, 1)

            def copy_h(i):
                act.wait_ge(s_h, i + 1)
                if not isinstance(i, int) or i >= 1:
                    act.wait_ge(s_hT, i)
                nc.scalar.activation(h_sb[:, 0:HALF], p_h[:, 0:HALF], ACT.Copy).then_inc(s_hsa, 1)

            def copy_fxT(i):
                act.wait_ge(s_fT, i + 1)
                if not isinstance(i, int) or i >= 1:
                    act.wait_ge(s_h, i)
                nc.scalar.activation(fxT, p_xT, ACT.Copy).then_inc(s_fTs, 1)

            copy_fxT(0)
            copy_h(0)
            copy_fxT(1)
            for i in range(FFN_RING):
                relu_hT(i, i)
                copy_h(i + 1)
                copy_fxT(i + 2)
            with act.Fori(1, SLOT_TILES // FFN_RING - 1) as k:
                for u in range(FFN_RING):
                    i = k * FFN_RING + u
                    relu_hT(i, u)
                    copy_h(i + 1)
                    copy_fxT(i + 2)
            for i in range(SLOT_TILES - FFN_RING, SLOT_TILES):
                relu_hT(i, i % FFN_RING)
                if i + 1 < SLOT_TILES:
                    copy_h(i + 1)
                if i + 2 < SLOT_TILES:
                    copy_fxT(i + 2)

        @block.tensor
        def _(pe):
            pe.wait_ge(s_wsq, 2)
            pe.wait_ge(s_const, 7)
            for k in range(DK):
                last = nc.tensor.matmul(p_S[:, 0:D], ones[:, :], xn[:, 0, k, :], start=k == 0, stop=k == DK - 1)
            last.then_inc(s_norm, 1)

            def transpose_xn(t, slot, ready, transposed):
                pe.wait_ge(ready, t + 1)
                for j in range(CT):
                    for k in range(DK):
                        last = nc.tensor.transpose(p_T[slot][:, j, k, :], xn[:, slot, j, k * P:(k + 1) * P], ident[:, :])
                last.then_inc(transposed, 1)

            def project(t, slot):
                pe.wait_ge(s_Ts, t + 1)
                if not isinstance(t, int) or t >= 2:
                    pe.wait_ge(s_lo, t - 1)
                for j in range(CT):
                    for k in range(DK):
                        last = nc.tensor.matmul(p_agg[slot][:, j, 0:D], xnT[:, slot, j, k, :], w_sb[:, k, :],
                                                start=k == 0, stop=k == DK - 1)
                last.then_inc(s_H, 1)

            pe.wait_ge(s_wscaled, 1)
            transpose_xn(0, 0, s_xn, s_T)
            transpose_xn(1, 1, s_xn, s_T)
            project(0, 0)
            transpose_xn(2, 0, s_xn, s_T)
            project(1, 1)
            with pe.Fori(1, (CHUNKS - 1) // 2) as r:
                for u in range(2):
                    transpose_xn(r * 2 + (u + 1), 1 - u, s_xn, s_T)
                    project(r * 2 + u, u)
            project(CHUNKS - 1, 0)

            pe.wait_ge(s_lo, CHUNKS)
            pe.wait_ge(s_hi, 2 * CHUNKS)

            def aggregate(c, k_load, buf, slot, k0, k1, j):
                for k in range(k0, k1):
                    nc.tensor.matmul(p_agg[slot][:, j, :], adj_half[buf][:, k, j * P:(j + 1) * P, 1],
                                     h_parts[:, k, :, :], start=k == 0, stop=k == TILES - 1)

            def flags(c, slot):
                pe.wait_ge(s_chka, c + 1)
                pe.wait_ge(s_chkv, c + 1)
                nc.tensor.matmul(p_S[0:1, 0:2], ones[:, 0:1], low_any[:, slot, :], start=True, stop=True).then_inc(s_flag, 1)

            def settle(c, buf, slot):
                pe.wait_ge(s_redo, c + 1)
                pe.nop(nofuse=True)
                again = pe.value_load(redo[0:1, 0:1], min_val=0, max_val=1)
                with pe.If(again > 0):
                    for j in range(CT):
                        for k in range(TILES):
                            nc.tensor.matmul(p_agg[slot][:, j, 0:D], adj_f32[buf][:, k, j * P:(j + 1) * P],
                                             h_full[:, k, :], start=k == 0, stop=k == TILES - 1, skip_group_check=True)
                        nc.tensor.matmul(p_agg[slot][:, j, D:2 * D], zeros[:, 0:P], zeros[:, :],
                                         start=False, stop=True, skip_group_check=True)
                nc.tensor.matmul(p_S[0:1, 8:9], ones[:, 0:1], ones[:, 0:1], start=True, stop=True).then_inc(s_agg, 1)

            def router(c, slot):
                pe.wait_ge(s_T2s, c + 1)
                for j in range(CT):
                    for k in range(DK):
                        last = nc.tensor.matmul(p_log[slot][:, j, :], xnT[:, slot, j, k, :], wg_sb[:, k, :],
                                                start=k == 0, stop=k == DK - 1)
                last.then_inc(s_log, 1)

            def chunk(c, k_load, buf, slot):
                pe.wait_ge(s_adj[buf], 16 * k_load)
                pe.wait_ge(s_free, c + 1)
                aggregate(c, k_load, buf, slot, 0, TILES, 0)
                flags(c, slot)
                aggregate(c, k_load, buf, slot, 0, TILES, 1)

            chunk(0, 1, 0, 0)
            settle(0, 0, 0)
            with pe.Fori(0, (CHUNKS - 1) // GNN_UNROLL) as r:
                for u in range(GNN_UNROLL):
                    c = r * GNN_UNROLL + (u + 1)
                    buf, slot = (u + 1) % ADJ_BUFS, (u + 1) % 2
                    chunk(c, r * 2 + ((u + 1) // ADJ_BUFS + 1), buf, slot)
                    transpose_xn(c - 1, 1 - slot, s_xn2, s_T2)
                    settle(c, buf, slot)
                    router(c - 1, 1 - slot)
            last_slot = (CHUNKS - 1) % 2
            transpose_xn(CHUNKS - 1, last_slot, s_xn2, s_T2)
            router(CHUNKS - 1, last_slot)

            pe.wait_ge(s_onehot, 1)
            pe.wait_ge(s_T2s, CHUNKS)
            nc.tensor.matmul(p_rank, earlier[:, :], onehot_f, start=True, stop=True).then_inc(s_rank, 1)
            nc.tensor.matmul(p_count, ones[:, :], onehot_f, start=True, stop=True).then_inc(s_rank, 1)
            pe.wait_ge(s_masks, 1)
            for k in range(TILES):
                last = nc.tensor.matmul(p_S[:, 0:2 * SLOT_TILES], slot_mask[:, k, :], tile_mask[:, k, :],
                                        start=k == 0, stop=k == TILES - 1)
            last.then_inc(s_slots, 1)

            def transpose_fx(i):
                pe.wait_ge(s_fx, i + 1)
                if not isinstance(i, int) or i >= 1:
                    pe.wait_ge(s_fTs, i)
                for k in range(DK):
                    last = nc.tensor.transpose(p_xT[:, k, :], fx[:, k * P:(k + 1) * P], ident[:, :])
                last.then_inc(s_fT, 1)

            def weights_at(i):
                e = pe.value_load(expert_no[0:1, bass.ds(i, 1)], min_val=0, max_val=E - 1)
                pe.wait_ge(s_w[0], 16 * (e // 2) + 16)
                pe.wait_ge(s_w[1], 16 * ((e + 1) // 2) + 16)
                return pe.snap(e * EXPERT_WORDS)

            def hidden(i, at):
                pe.wait_ge(s_fTs, i + 1)
                if not isinstance(i, int) or i >= 1:
                    pe.wait_ge(s_hsa, i)
                    pe.wait_ge(s_hsv, i)
                for n in range(HID // 512):
                    for k in range(DK):
                        last = nc.tensor.matmul(p_h[:, n * 512:(n + 1) * 512], fxT[:, k, :],
                                                arena[:, bass.ds(at + (k * HID + n * 512), 512)],
                                                start=k == 0, stop=k == DK - 1)
                last.then_inc(s_h, 1)

            def transpose_h(i):
                pe.wait_ge(s_hsa, i + 1)
                pe.wait_ge(s_hsv, i + 1)
                if not isinstance(i, int) or i >= 1:
                    pe.wait_ge(s_hTa, i)
                    pe.wait_ge(s_hTv, i)
                for j in range(HB):
                    last = nc.tensor.transpose(p_hT[:, j, :], h_sb[:, j * P:(j + 1) * P], ident[:, :])
                last.then_inc(s_hT, 1)

            def output(i, at, j0, j1):
                if j0 == 0:
                    pe.wait_ge(s_hTa, i + 1)
                    pe.wait_ge(s_hTv, i + 1)
                    if not isinstance(i, int) or i >= 1:
                        pe.wait_ge(s_yb, i)
                for j in range(j0, j1):
                    last = nc.tensor.matmul(p_y[:, 0:D], hT_sb[:, j, :],
                                            arena[:, bass.ds(at + (DK * HID + j * D), D)],
                                            start=j == 0, stop=j == HB - 1)
                if j1 == HB:
                    last.then_inc(s_y, 1)

            pe.wait_ge(s_table, 1)
            transpose_fx(0)
            hidden(0, weights_at(0))
            transpose_fx(1)

            def tile(i, has1, has2):
                transpose_h(i)
                if has1:
                    hidden(i + 1, weights_at(i + 1))
                at = weights_at(i)
                output(i, at, 0, HB // 2)
                if has2:
                    transpose_fx(i + 2)
                output(i, at, HB // 2, HB)

            for i in range(FFN_RING):
                tile(i, True, True)
            with pe.Fori(1, SLOT_TILES // FFN_RING - 1) as r:
                for u in range(FFN_RING):
                    tile(r * FFN_RING + u, True, True)
            for i in range(SLOT_TILES - FFN_RING, SLOT_TILES):
                tile(i, i + 1 < SLOT_TILES, i + 2 < SLOT_TILES)

        @block.vector
        def _(dve):
            chain = Chain(dve, s_dve)
            step = chain.step
            dve.wait_ge(s_wg, 16)
            for k in range(DK):
                nc.vector.tensor_tensor(xn[:, 0, k, :], w_sb[:, k, :], w_sb[:, k, :], ALU.mult).then_inc(s_wsq, 1)
            bits = lo_sum[:, 0, :].bitcast(I32)
            scale = lo_sum[:, 1, :]
            inv_bits = inv_scale[:, :].bitcast(I32)
            dve.wait_ge(s_norm, 1)
            step(nc.vector.tensor_copy(lo_sum[:, 0, :], p_S[:, 0:D]))
            step(nc.vector.tensor_scalar(bits, bits, 23, None, ALU.logical_shift_right))
            step(nc.vector.tensor_scalar(bits, bits, 1.0, None, ALU.add))
            step(nc.vector.tensor_scalar(bits, bits, 1, None, ALU.logical_shift_right))
            step(nc.vector.tensor_scalar(scale.bitcast(I32), bits, -1.0, float(SCALE_EXP), ALU.mult, ALU.add))
            step(nc.vector.tensor_scalar(scale.bitcast(I32), scale.bitcast(I32), 23, None, ALU.logical_shift_left))
            step(nc.vector.tensor_scalar(inv_bits, bits, float(INV_EXP), None, ALU.add))
            step(nc.vector.tensor_scalar(inv_bits, inv_bits, 23, None, ALU.logical_shift_left))
            nc.vector.tensor_tensor(w_sb[:, :, :], w_sb[:, :, :], scale.unsqueeze(1).to_broadcast([P, DK, D]),
                                    ALU.mult).then_inc(s_wscaled, 1)

            half = TILES // 2
            for t in range(TILES):
                if t % half == 0:
                    dve.wait_ge(s_x[t // half], 16)
                chain.mark(nc.vector.bn_stats(stats[:, t, :], x_sb[:, t, :]))
            chain.wait()
            for t in range(TILES):
                chain.mark(nc.vector.bn_aggr(mv[:, t, :], stats[:, t, :]))
            chain.wait()
            nc.vector.tensor_scalar(rstd[:, :], mv[:, :, 1], EPS, None, ALU.add).then_inc(s_var, 1)
            dve.wait_ge(s_std, 1)
            step(nc.vector.reciprocal(rstd[:, :], rstd[:, :]))
            step(nc.vector.scalar_tensor_tensor(out=nmr[:, :], in0=mv[:, :, 0], scalar=-1.0, in1=rstd[:, :],
                                                op0=ALU.mult, op1=ALU.mult))
            dve.wait_ge(s_wscaled, 1)

            def normalize(t, slot):
                if not isinstance(t, int) or t >= 2:
                    dve.wait_ge(s_T, t - 1)
                elif t == 0:
                    dve.wait_ge(s_norm, 1)
                for j in range(CT):
                    last = nc.vector.tensor_scalar(xn[:, slot, j, :], x_sb[:, bass.ds(t * CT + j, 1), :].rearrange("p k d -> p (k d)"),
                                                   rstd[:, bass.ds(t * CT + j, 1)], nmr[:, bass.ds(t * CT + j, 1)],
                                                   ALU.mult, ALU.add)
                last.then_inc(s_xn, 1)

            def low_part(t, slot):
                dve.wait_ge(s_hi, 2 * t + 2)
                nc.vector.tensor_tensor(h_parts[:, bass.ds(t * CT, CT), 1, :], p_agg[slot][:, :, 0:D],
                                        h_parts[:, bass.ds(t * CT, CT), 0, :], ALU.subtract).then_inc(s_lo, 1)

            normalize(0, 0)
            normalize(1, 1)
            normalize(2, 0)
            low_part(0, 0)
            with dve.Fori(0, (CHUNKS - 3) // 2) as r:
                for u in range(2):
                    normalize(r * 2 + (u + 3), 1 - u)
                    low_part(r * 2 + (u + 1), 1 - u)
            low_part(CHUNKS - 2, 1)
            low_part(CHUNKS - 1, 0)

            def check(c, k_load, buf, slot):
                dve.wait_ge(s_adj[buf], 16 * k_load)
                nc.vector.tensor_reduce(low_any[:, slot, 1:2], adj_bits[buf][:, ACT_PART:CHUNK_WORDS, 0],
                                        AX.X, ALU.max).then_inc(s_chkv, 1)

            def decide(c):
                dve.wait_ge(s_flag, c + 1)
                nc.vector.tensor_reduce(low_top[:, :], p_S[0:1, 0:2], AX.X, ALU.max).then_inc(s_lowtop, 1)
                dve.wait_ge(s_lowtop, c + 1)
                nc.vector.tensor_scalar(redo[:, :], low_top[:, :], 0.0, None, ALU.is_gt).then_inc(s_redo, 1)

            STEPS = 1 + 2 * CT + 1 + 1
            finish_base = chain.n

            def finish(c, slot):
                chain.enter(c * STEPS + finish_base)
                r = rows[:, slot, :, 0:D]
                dve.wait_ge(s_losum, c + 1)
                dve.wait_ge(s_rowfree, c + 1)
                nc.vector.tensor_tensor(r, p_agg[slot][:, :, 0:D], lo_sum[:, :, :], ALU.add).then_inc(s_free, 1)
                dve.wait_ge(s_free, c + 3)
                step(nc.vector.tensor_tensor(r, r, inv_scale[:, :].unsqueeze(1).to_broadcast([P, CT, D]), ALU.mult))
                dve.wait_ge(s_xb, CT * c + CT)
                step(nc.vector.tensor_tensor(r, r, x_sb[:, bass.ds(c * CT, CT), :], ALU.add))
                for j in range(CT):
                    chain.mark(nc.vector.bn_stats(stats2[:, j, :], rows[:, slot, j, 0:D]))
                chain.wait()
                dve.nop(nofuse=True)
                for j in range(CT):
                    chain.mark(nc.vector.bn_aggr(mv2[:, j, :], stats2[:, j, :]))
                chain.wait()
                nc.vector.tensor_scalar(mv2[:, :, 1], mv2[:, :, 1], EPS, None, ALU.add).then_inc(s_var2, 1)
                dve.wait_ge(s_std2, c + 1)
                step(nc.vector.reciprocal(rows[:, slot, :, D], std2[:, :]))
                nc.vector.scalar_tensor_tensor(out=rows[:, slot, :, D + 1], in0=mv2[:, :, 0], scalar=-1.0,
                                               in1=rows[:, slot, :, D], op0=ALU.mult, op1=ALU.mult).then_inc(s_row, 1)
                dve.wait_ge(s_row, c + 1)
                for j in range(CT):
                    last = nc.vector.tensor_scalar(xn[:, slot, j, :], rows[:, slot, j, 0:D], rows[:, slot, j, D:D + 1],
                                                   rows[:, slot, j, D + 1:D + 2], ALU.mult, ALU.add)
                last.then_inc(s_xn2, 1)

            def keep_logits(c, slot):
                dve.wait_ge(s_log, c + 1)
                nc.vector.tensor_tensor(logits[:, bass.ds(c * CT, CT), :], p_log[slot], bg_sb[:, :, :],
                                        ALU.add).then_inc(s_logs, 1)

            dve.wait_ge(s_lo, CHUNKS)
            dve.sem_inc(s_free, 2)
            dve.wait_ge(s_small, SMALL)
            check(0, 1, 0, 0)
            decide(0)
            with dve.Fori(0, (CHUNKS - 1) // GNN_UNROLL) as r:
                for u in range(GNN_UNROLL):
                    c = r * GNN_UNROLL + (u + 1)
                    check(c, r * 2 + ((u + 1) // ADJ_BUFS + 1), (u + 1) % ADJ_BUFS, (u + 1) % 2)
                    decide(c)
                    finish(c - 1, u % 2)
                    keep_logits(c - 1, u % 2)
            finish(CHUNKS - 1, (CHUNKS - 1) % 2)
            keep_logits(CHUNKS - 1, (CHUNKS - 1) % 2)
            chain.enter(finish_base + CHUNKS * STEPS)
            dve.wait_ge(s_logs, CHUNKS)

            def over_experts(a):
                return a.unsqueeze(2).to_broadcast([P, TILES, E])

            step(nc.vector.tensor_reduce(top, logits[:, :, :], AX.X, ALU.max))
            nc.vector.tensor_tensor(soft, logits[:, :, :], over_experts(top), ALU.subtract).then_inc(s_soft, 1)
            step(nc.vector.tensor_tensor(pick, logits[:, :, :], over_experts(top), ALU.is_equal))
            step(nc.vector.tensor_tensor(pick, pick, down[:, :].unsqueeze(1).to_broadcast([P, TILES, E]), ALU.mult))
            step(nc.vector.tensor_reduce(first, pick, AX.X, ALU.max))
            step(nc.vector.tensor_scalar(is_token[:, :], padding[:, :], -1.0, 1.0, ALU.mult, ALU.add))
            step(nc.vector.tensor_tensor(pick, pick, over_experts(first), ALU.is_equal))
            nc.vector.tensor_tensor(onehot, pick.rearrange("p k e -> p e k"),
                                    is_token[:, :].unsqueeze(1).to_broadcast([P, E, TILES]), ALU.mult).then_inc(s_onehot, 1)
            step(nc.vector.memset(ones_w, 1.0))
            step(nc.vector.memset(running[:, 0:1], 0.0))
            dve.wait_ge(s_exp, 1)
            step(nc.vector.tensor_reduce(score, soft, AX.X, ALU.add))
            step(nc.vector.reciprocal(score, score))
            dve.wait_ge(s_rank, 2)
            step(nc.vector.tensor_tensor_scan(running[:, 1:1 + E * TILES], ones_w, p_count, 0.0, ALU.mult, ALU.add))
            run_start = running[:, 0:E * TILES].rearrange("p (e k) -> p e k", e=E)
            run_end = running[:, 1:1 + E * TILES].rearrange("p (e k) -> p e k", e=E)
            step(nc.vector.tensor_tensor(tiles_f, run_end[:, :, TILES - 1], run_start[:, :, 0], ALU.subtract))
            step(nc.vector.tensor_scalar(tiles_i, tiles_f, float(P - 1), None, ALU.add))
            step(nc.vector.tensor_scalar(tiles_i, tiles_i, P.bit_length() - 1, None, ALU.logical_shift_right))
            step(nc.vector.tensor_copy(tiles_f, tiles_i))
            step(nc.vector.tensor_tensor_scan(tile_end, ones_w[:, 0:E], tiles_f, 0.0, ALU.mult, ALU.add))
            step(nc.vector.tensor_tensor(start_e, tile_end, tiles_f, ALU.subtract))
            step(nc.vector.scalar_tensor_tensor(out=start_e, in0=start_e, scalar=float(P), in1=run_start[:, :, 0],
                                                op0=ALU.mult, op1=ALU.subtract))
            step(nc.vector.tensor_tensor(slot_no, run_start, start_e.unsqueeze(2).to_broadcast([P, E, TILES]), ALU.add))
            step(nc.vector.tensor_tensor(slot_no, slot_no, p_rank.rearrange("p (e k) -> p e k", e=E), ALU.add))
            step(nc.vector.tensor_tensor(slot_no, slot_no, onehot, ALU.mult))
            step(nc.vector.tensor_reduce(pos, slot_no.rearrange("p e k -> p k e"), AX.X, ALU.add))
            step(nc.vector.scalar_tensor_tensor(out=pos, in0=padding[:, :], scalar=float(SLOT_TILES * P), in1=pos,
                                                op0=ALU.mult, op1=ALU.add))
            step(nc.vector.tensor_copy(pos_i[:, 2, :], pos))
            step(nc.vector.tensor_scalar(pos_i[:, 0, :], pos_i[:, 2, :], P.bit_length() - 1, None, ALU.logical_shift_right))
            step(nc.vector.tensor_scalar(pos_i[:, 1, :], pos_i[:, 2, :], P - 1, None, ALU.bitwise_and))
            step(nc.vector.tensor_copy(pos_f, pos_i[:, 0:2, :]))
            def over(a, n):
                return a.unsqueeze(2).to_broadcast([P, TILES, n])

            in_tile, scored = tile_mask[:, :, 0:SLOT_TILES], tile_mask[:, :, SLOT_TILES:2 * SLOT_TILES]
            step(nc.vector.tensor_tensor(slot_mask, iota_slot[:, :].unsqueeze(1).to_broadcast([P, TILES, P]),
                                         over(pos_f[:, 1, :], P), ALU.is_equal))
            step(nc.vector.tensor_tensor(in_tile, iota_tile[:, :].unsqueeze(1).to_broadcast([P, TILES, SLOT_TILES]),
                                         over(pos_f[:, 0, :], SLOT_TILES), ALU.is_equal))
            step(nc.vector.tensor_tensor(scored, in_tile, over(score, SLOT_TILES), ALU.mult))
            nc.vector.tensor_tensor(in_tile, in_tile, over(token_no[:, :], SLOT_TILES), ALU.mult).then_inc(s_masks, 1)
            step(nc.vector.tensor_tensor(ended, iota_tile[0:1, :].unsqueeze(2).to_broadcast([1, SLOT_TILES, E]),
                                         tile_end[0:1, :].unsqueeze(1).to_broadcast([1, SLOT_TILES, E]), ALU.is_ge))
            step(nc.vector.tensor_reduce(expert_f, ended, AX.X, ALU.add))
            step(nc.vector.tensor_scalar(expert_no[:, :], expert_f, float(E - 1), None, ALU.min))
            dve.wait_ge(s_slots, 1)
            step(nc.vector.tensor_copy(slot_score[:, :], p_S[:, SLOT_TILES:2 * SLOT_TILES]))
            step(nc.vector.tensor_scalar(row_f, p_S[:, 0:SLOT_TILES], 1.0, SKIP, ALU.is_lt, ALU.mult))
            nc.vector.scalar_tensor_tensor(out=slot_row[:, :], in0=p_S[:, 0:SLOT_TILES], scalar=-1.0, in1=row_f,
                                           op0=ALU.add, op1=ALU.add).then_inc(s_table, 1)
            dve.wait_ge(s_table, 1)
            dve.wait_ge(s_w[1], 16)

            HALF = HID // 2

            def relu_hT(i, slot):
                dve.wait_ge(s_hT, i + 1)
                if not isinstance(i, int) or i >= 1:
                    dve.wait_ge(s_y, i)
                dve.wait_ge(s_now, 3 * i + 3)
                for j in range(HB // 2, HB):
                    last = nc.vector.tensor_scalar(hT_sb[:, j, :], p_hT[:, j, :], b1_now[:, slot, j:j + 1], 0.0,
                                                   ALU.add, ALU.max)
                last.then_inc(s_hTv, 1)

            def copy_h(i):
                dve.wait_ge(s_h, i + 1)
                if not isinstance(i, int) or i >= 1:
                    dve.wait_ge(s_hT, i)
                nc.vector.tensor_copy(h_sb[:, HALF:HID], p_h[:, HALF:HID]).then_inc(s_hsv, 1)

            def normalize_rows(i, k, slot):
                dve.wait_ge(s_got[slot], 16 * k + 16)
                if not isinstance(i, int) or i >= 1:
                    dve.wait_ge(s_fT, i)
                g = got[slot]
                nc.vector.tensor_scalar(fx, g[:, 0:D], g[:, D:D + 1], g[:, D + 1:D + 2], ALU.mult, ALU.add).then_inc(s_fx, 1)

            def finish_rows(i, k, slot):
                e = dve.value_load(expert_no[0:1, bass.ds(i, 1)], min_val=0, max_val=E - 1)
                dve.wait_ge(s_y, i + 1)
                nc.vector.tensor_tensor(yb, p_y[:, 0:D], b2_sb[:, bass.ds(e, 1), :].rearrange("p e d -> p (e d)"),
                                        ALU.add).then_inc(s_yb, 1)
                dve.wait_ge(s_yb, i + 1)
                if not isinstance(k, int) or k >= 1:
                    dve.wait_ge(s_out[slot], 16 * k)
                nc.vector.scalar_tensor_tensor(out=done[slot], in0=yb, scalar=score_now[:, slot:slot + 1],
                                               in1=got[slot][:, 0:D], op0=ALU.mult, op1=ALU.add).then_inc(s_done, 1)

            normalize_rows(0, 0, 0)
            copy_h(0)
            normalize_rows(1, 0, 1)
            for i in range(FFN_RING):
                relu_hT(i, i)
                copy_h(i + 1)
                normalize_rows(i + 2, (i + 2) // FFN_RING, (i + 2) % FFN_RING)
                finish_rows(i, 0, i)
            with dve.Fori(1, SLOT_TILES // FFN_RING - 1) as k:
                for u in range(FFN_RING):
                    i = k * FFN_RING + u
                    relu_hT(i, u)
                    copy_h(i + 1)
                    normalize_rows(i + 2, k + (u + 2) // FFN_RING, (u + 2) % FFN_RING)
                    finish_rows(i, k, u)
            for i in range(SLOT_TILES - FFN_RING, SLOT_TILES):
                relu_hT(i, i % FFN_RING)
                if i + 1 < SLOT_TILES:
                    copy_h(i + 1)
                if i + 2 < SLOT_TILES:
                    normalize_rows(i + 2, (i + 2) // FFN_RING, (i + 2) % FFN_RING)
                finish_rows(i, i // FFN_RING, i % FFN_RING)


def kernel(x, adj, L0_gnn_W, L0_gnn_b, L0_ffn_Wg, L0_ffn_bg, L0_ffn_W1, L0_ffn_b1, L0_ffn_W2, L0_ffn_b2):
    import numpy as np
    import concourse.bacc as bacc
    from concourse.bass_utils import run_bass_kernel_spmd

    x, adj = np.asarray(x), np.asarray(adj)
    x_pad = np.zeros((NPAD, D), x.dtype)
    x_pad[:N] = x
    adj_t = np.zeros((NPAD, NPAD), adj.dtype)
    adj_t[:N, :N] = adj.T
    w1, w2 = np.asarray(L0_ffn_W1), np.asarray(L0_ffn_W2)
    arrays = {
        "x": x_pad.reshape(TILES, P, D).transpose(1, 0, 2),
        "adj": adj_t.reshape(TILES, P, CHUNKS, CT * P).transpose(2, 1, 0, 3).reshape(CHUNKS, P, CHUNK_WORDS),
        "w_gnn": np.asarray(L0_gnn_W).transpose(1, 0, 2).reshape(DK, P, D).transpose(1, 0, 2),
        "b_gnn": np.asarray(L0_gnn_b).reshape(1, D),
        "w_gate": np.asarray(L0_ffn_Wg).reshape(DK, P, E).transpose(1, 0, 2),
        "b_gate": np.asarray(L0_ffn_bg).reshape(1, E),
        "w_exp": np.concatenate([w1.reshape(E, DK, P, HID).transpose(0, 2, 1, 3).reshape(E, P, DK * HID),
                                 w2.reshape(E, HB, P, D).transpose(0, 2, 1, 3).reshape(E, P, HB * D)], axis=2),
        "b1": np.asarray(L0_ffn_b1).reshape(E, HB, P).transpose(2, 0, 1),
        "b2": np.asarray(L0_ffn_b2).reshape(1, E * D),
    }
    arrays = {name: np.ascontiguousarray(a) for name, a in arrays.items()}
    nc = bacc.Bacc("TRN2", target_bir_lowering=False, num_devices=1)
    args = [nc.dram_tensor(name, a.shape, mybir.dt.from_np(a.dtype), kind="ExternalInput").ap()
            for name, a in arrays.items()]
    out = nc.dram_tensor("out", (N, D), F32, kind="ExternalOutput").ap()
    build(nc, *args, out)
    r = run_bass_kernel_spmd(nc, [arrays], core_ids=[0])
    return r.results[0]["out"]
```

```python
from contextlib import ExitStack

import concourse.bass as bass
from concourse import mybir

ALU = mybir.AluOpType
ACT = mybir.ActivationFunctionType
AX = mybir.AxisListType
F32 = mybir.dt.float32
F16 = mybir.dt.float16
BF16 = mybir.dt.bfloat16
U16 = mybir.dt.uint16
I32 = mybir.dt.int32

P = 128
N = 3327
D = 256
DK = D // P
TILES = -(-N // P)
NPAD = TILES * P
CT = 2
CHUNKS = TILES // CT
CHUNK_WORDS = TILES * CT * P
E = 8
HID = 1024
HB = HID // P
SLOT_TILES = (N + E * (P - 1)) // P
ROW = D + 4
EPS = 1e-5
ADJ_BUFS = 3
GNN_UNROLL = 2 * ADJ_BUFS
AHEAD = 4
FIRST_TILES = AHEAD * CT
FFN_RING = 3
EXPERT_WORDS = DK * HID + HB * D
EARLY = 1
FLAGS_AT = 8
TRANSPOSE_AT = 10
ROUTER_AT = 16
ACT_PART = 4096
SKIP = 100000.0
SCALE_EXP = 201
INV_EXP = 254 - SCALE_EXP

assert (CHUNKS - 1) % GNN_UNROLL == 0 and SLOT_TILES % FFN_RING == 0


class Chain:

    def __init__(self, eng, sem):
        self.eng, self.sem, self.base, self.n = eng, sem, 0, 0

    def enter(self, base):
        self.base, self.n = base, 0

    def mark(self, ins):
        self.n += 1
        ins.then_inc(self.sem, 1)

    def wait(self):
        self.eng.wait_ge(self.sem, self.base + self.n)

    def step(self, ins):
        self.mark(ins)
        self.wait()


def build(nc, x, adj, w_gnn, b_gnn, w_gate, b_gate, w_exp, b1, b2, out):
    with ExitStack() as ctx:
        def sb(name, shape, dt=F32):
            return ctx.enter_context(nc.sbuf_tensor(name, shape, dt))

        def ps(name, shape):
            return ctx.enter_context(nc.psum_tensor(name, shape, F32))

        def sem(name):
            return ctx.enter_context(nc.semaphore(name))

        x2_rows = nc.dram_tensor("x2_rows", (NPAD, ROW), F32, kind="Internal").ap()

        ADJ0 = EARLY * EXPERT_WORDS
        HP0 = ADJ0 + ADJ_BUFS * CHUNK_WORDS
        arena = sb("arena", [P, max(HP0 + TILES * D + ACT_PART // 2, E * EXPERT_WORDS)])
        adj_sb = [arena[:, ADJ0 + s * CHUNK_WORDS:ADJ0 + (s + 1) * CHUNK_WORDS] for s in range(ADJ_BUFS)]
        adj_f32 = [a.rearrange("p (k n) -> p k n", n=CT * P) for a in adj_sb]
        adj_half = [a.bitcast(BF16).rearrange("p (k n two) -> p k n two", n=CT * P, two=2) for a in adj_sb]
        adj_bits = [a.bitcast(U16).rearrange("p (w two) -> p w two", two=2) for a in adj_sb]
        junk = arena[:, HP0 + TILES * D:HP0 + TILES * D + ACT_PART // 2].bitcast(BF16)
        h_parts = arena[:, HP0:HP0 + TILES * D].bitcast(F16).rearrange("p (k s d) -> p k s d", s=2, d=D)
        x_sb = sb("x_sb", [P, TILES, D])
        reuse = sb("reuse", [P, TILES * D])
        h_full = reuse[:, :].rearrange("p (k d) -> p k d", d=D)

        ident = sb("ident", [P, P])
        ones = sb("ones", [P, P])
        zeros = sb("zeros", [P, D])
        earlier = sb("earlier", [P, P])
        w_sb = sb("w_sb", [P, DK, D])
        wg_sb = sb("wg_sb", [P, DK, E])
        bg_sb = sb("bg_sb", [P, CT, E])
        b1_sb = sb("b1_sb", [P, E, HB])
        b_bc = sb("b_bc", [P, D])
        inv_scale = sb("inv_scale", [P, D])
        stats = sb("stats", [P, AHEAD, CT, 6])
        mv = sb("mv", [P, AHEAD, CT, 2])
        rstd = sb("rstd", [P, AHEAD, CT])
        nmr = sb("nmr", [P, AHEAD, CT])
        xn = sb("xn", [P, 2, CT, D])
        xnT = sb("xnT", [P, 2, CT, DK, P])
        rows = sb("rows", [P, 2, CT, ROW])
        lo_sum = sb("lo_sum", [P, CT, D])
        stats2 = sb("stats2", [P, CT, 6])
        mv2 = sb("mv2", [P, CT, 2])
        minus_half = sb("minus_half", [P, TILES])
        logits = sb("logits", [P, TILES, E])
        low_any = sb("low_any", [P, 2, 2])
        low_top = sb("low_top", [1, 1])
        redo = sb("redo", [1, 1], I32)

        iota_tile = sb("iota_tile", [P, SLOT_TILES])
        iota_slot = sb("iota_slot", [P, P])
        token_no = sb("token_no", [P, TILES])
        padding = sb("padding", [P, TILES])
        is_token = sb("is_token", [P, TILES])
        down = sb("down", [P, E])
        slot_row = sb("slot_row", [P, SLOT_TILES], I32)
        slot_score = sb("slot_score", [P, SLOT_TILES])
        expert_no = sb("expert_no", [1, SLOT_TILES], I32)
        row_in = sb("row_in", [P, FFN_RING], I32)
        row_out = sb("row_out", [P, FFN_RING], I32)
        score_now = sb("score_now", [P, FFN_RING])
        b1_now = sb("b1_now", [P, FFN_RING, HB])

        class Cut:
            def __init__(self, ap, size):
                self.ap, self.at, self.size = ap, 0, size

            def take(self, n):
                self.at += n
                assert self.at <= self.size
                return self.ap[:, self.at - n:self.at]

        cut = Cut(x_sb[:, :, :].rearrange("p k d -> p (k d)"), TILES * D)
        slot_mask = cut.take(TILES * P).rearrange("p (k s) -> p k s", s=P)
        tile_mask = cut.take(TILES * 2 * SLOT_TILES).rearrange("p (k w) -> p k w", w=2 * SLOT_TILES)
        soft = cut.take(TILES * E).rearrange("p (k e) -> p k e", e=E)
        pick = cut.take(TILES * E).rearrange("p (k e) -> p k e", e=E)
        onehot_f = cut.take(E * TILES)
        onehot = onehot_f.rearrange("p (e k) -> p e k", e=E)
        slot_no = cut.take(E * TILES).rearrange("p (e k) -> p e k", e=E)
        ones_w = cut.take(E * TILES)
        top = cut.take(TILES)
        first = cut.take(TILES)
        score = cut.take(TILES)
        running = cut.take(1 + E * TILES)
        tiles_i = cut.take(E).bitcast(I32)
        tiles_f = cut.take(E)
        tile_end = cut.take(E)
        start_e = cut.take(E)
        pos = cut.take(TILES)
        pos_i = cut.take(3 * TILES).bitcast(I32).rearrange("p (w k) -> p w k", w=3)
        pos_f = cut.take(2 * TILES).rearrange("p (w k) -> p w k", w=2)
        cut = Cut(xnT[:, :, :, :, :].rearrange("p s c k t -> p (s c k t)"), 2 * CT * D)
        ended = cut.take(SLOT_TILES * E)[0:1, :].rearrange("p (i e) -> p i e", e=E)
        expert_f = cut.take(SLOT_TILES)[0:1, :]
        row_f = cut.take(SLOT_TILES)

        cut2 = Cut(reuse, TILES * D)
        b2_sb = cut2.take(E * D).rearrange("p (e d) -> p e d", d=D)
        h_sb = cut2.take(HID)
        hT_sb = cut2.take(HID).rearrange("p (j t) -> p j t", t=P)
        got = [cut2.take(ROW) for _ in range(FFN_RING)]
        done = [cut2.take(D) for _ in range(FFN_RING)]
        fx = cut2.take(D)
        fxT = cut2.take(D).rearrange("p (k t) -> p k t", t=P)
        yb = cut2.take(D)

        p_agg = [ps(f"p_agg{s}", [P, CT, 512]) for s in range(2)]
        p_T = [ps(f"p_T{s}", [P, CT, DK, P]) for s in range(2)]
        p_S = ps("p_S", [P, 512])
        p_y = ps("p_y", [P, 512])
        p_log = [p_y[:, s * 64:s * 64 + CT * E].rearrange("p (c e) -> p c e", e=E) for s in range(2)]
        p_h = p_agg[0][:, :, :].rearrange("p c n -> p (c n)")
        p_hT = p_agg[1][:, :, :].rearrange("p c (j t) -> p (c j) t", t=P)
        p_xT = p_T[0][:, 0, :, :]
        p_rank, p_count = (t[:, :, :, :].rearrange("p c k t -> p (c k t)")[:, 0:E * TILES] for t in p_T)

        s_x = [sem(f"x_loaded{i}") for i in range(2)]
        s_wg = sem("w_gnn_loaded")
        s_small = sem("small_loaded")
        s_adj = [sem(f"adj_loaded{i}") for i in range(ADJ_BUFS)]
        s_w = [sem(f"weights_loaded{i}") for i in range(2)]
        s_const = sem("constants_made")
        s_pool = sem("pool_chain")
        s_dve = sem("dve_chain")
        s_wsq = sem("w_squared")
        s_norm = sem("column_norms_summed")
        s_wscaled = sem("w_scaled")
        s_ones = sem("ones_made")
        s_stats = sem("statistics_of_half_rows_ready")
        s_aggr = sem("means_and_variances_ready")
        s_var = sem("variances_ready")
        s_half = sem("minus_half_made")
        s_rstd = sem("rstds_ready")
        s_nmr = sem("means_times_rstds_ready")
        s_xn = sem("xn_ready")
        s_T = sem("xn_transposed")
        s_Ts = sem("xnT_in_sbuf")
        s_H = sem("h_summed")
        s_hi = sem("h_high_and_full_copied")
        s_lo = sem("h_low_copied")
        s_xb = sem("b_added_to_x")
        s_chkv = sem("low_halves_checked_dve")
        s_chka = sem("low_halves_checked_act")
        s_flag = sem("flags_summed")
        s_lowtop = sem("flags_reduced")
        s_redo = sem("redo_known")
        s_agg = sem("chunk_aggregated")
        s_losum = sem("low_sum_copied")
        s_free = sem("aggregate_read")
        s_var2 = sem("var2_ready")
        s_rstd2 = sem("rstd2_ready")
        s_xn2 = sem("xn2_ready")
        s_row = sem("rows_ready")
        s_stored = sem("rows_stored")
        s_rowfree = sem("row_slot_free")
        s_T2 = sem("xn2_transposed")
        s_T2s = sem("xn2T_in_sbuf")
        s_log = sem("logits_summed")
        s_logs = sem("logits_in_sbuf")
        s_soft = sem("softmax_argument_ready")
        s_exp = sem("exp_ready")
        s_onehot = sem("onehot_ready")
        s_rank = sem("ranks_summed")
        s_masks = sem("masks_ready")
        s_slots = sem("slots_summed")
        s_table = sem("tables_ready")
        s_clear = sem("gather_buffers_cleared")
        s_got = [sem(f"rows_gathered{i}") for i in range(FFN_RING)]
        s_now = sem("tile_columns_copied")
        s_fx = sem("ffn_xn_ready")
        s_fT = sem("ffn_xn_transposed")
        s_fTs = sem("ffn_xnT_in_sbuf")
        s_h = sem("hidden_summed")
        s_hsa = sem("hidden_copied_act")
        s_hsv = sem("hidden_copied_dve")
        s_hT = sem("hidden_transposed")
        s_hTa = sem("hiddenT_relu_act")
        s_hTv = sem("hiddenT_relu_dve")
        s_y = sem("ffn_summed")
        s_yb = sem("ffn_sum_read")
        s_done = sem("rows_finished")
        s_out = [sem(f"rows_scattered{i}") for i in range(FFN_RING)]
        SMALL = 16 * 4

        block = ctx.enter_context(nc.Block())

        @block.sync
        def _(sp):
            sp.dma_start(w_sb[:, :, :], w_gnn).then_inc(s_wg, 16)
            for i, (k0, k1) in enumerate(((0, FIRST_TILES), (FIRST_TILES, TILES))):
                sp.dma_start(x_sb[:, k0:k1, :], x[:, k0:k1, :]).then_inc(s_x[i], 16)
            for c in range(ADJ_BUFS):
                sp.dma_start(adj_sb[c], adj[c]).then_inc(s_adj[c], 16)

            def load_expert(e):
                if e >= 1:
                    sp.wait_ge(s_w[e % 2], 16 * ((e + 1) // 2))
                sp.dma_start(arena[:, e * EXPERT_WORDS:(e + 1) * EXPERT_WORDS], w_exp[e]).then_inc(s_w[e % 2], 16)

            def reload(c, buf):
                sp.wait_ge(s_agg, c - (ADJ_BUFS - 1))
                sp.dma_start(adj_sb[buf], adj[bass.ds(c, 1), :, :].rearrange("c p w -> p (c w)")).then_inc(s_adj[buf], 16)

            turns = (CHUNKS - ADJ_BUFS) // ADJ_BUFS
            with sp.Fori(0, turns) as r:
                for u in range(ADJ_BUFS):
                    reload(r * ADJ_BUFS + (ADJ_BUFS + u), u)
            for c in range(ADJ_BUFS + turns * ADJ_BUFS, CHUNKS):
                reload(c, c % ADJ_BUFS)
            for e in range(EARLY):
                load_expert(e)
            sp.wait_ge(s_agg, CHUNKS)
            sp.dma_start(b2_sb.rearrange("p e d -> p (e d)"), b2.to_broadcast([P, E * D])).then_inc(s_w[1], 16)
            for e in range(EARLY, E):
                load_expert(e)

        @block.gpsimd
        def _(pool):
            pool.memset(ones[:, :], 1.0).then_inc(s_ones, 1)
            pool.dma_start(wg_sb[:, :, :], w_gate).then_inc(s_small, 16)
            pool.dma_start(bg_sb[:, :, :], b_gate.unsqueeze(0).to_broadcast([P, CT, E])).then_inc(s_small, 16)
            pool.dma_start(b1_sb[:, :, :], b1).then_inc(s_small, 16)
            pool.dma_start(b_bc[:, :], b_gnn.to_broadcast([P, D])).then_inc(s_small, 16)
            chain = Chain(pool, s_pool)
            chain.mark(pool.memset(ident[:, :], 0.0))
            chain.mark(pool.memset(zeros[:, :], 0.0))
            chain.mark(pool.memset(padding[:, :], 0.0))
            chain.mark(pool.memset(rows[:, :, :, D:ROW], 0.0))
            chain.wait()
            CONSTANTS = chain.n
            pool.wait_ge(s_ones, 1)
            pool.affine_select(out=ident[:, :], in_=ident[:, :], compare_op=ALU.not_equal, fill=1.0,
                               base=0, pattern=[[-1, P]], channel_multiplier=1).then_inc(s_const, 1)
            pool.affine_select(out=earlier[:, :], in_=ones[:, :], compare_op=ALU.is_gt, fill=0.0,
                               base=0, pattern=[[1, P]], channel_multiplier=-1).then_inc(s_const, 1)
            pool.affine_select(out=padding[:, :], in_=padding[:, :], compare_op=ALU.is_gt, fill=1.0,
                               base=N, pattern=[[-P, TILES]], channel_multiplier=-1).then_inc(s_const, 1)
            for table, pattern, base, step in ((iota_tile, [[1, SLOT_TILES]], 0, 0), (iota_slot, [[1, P]], 0, 0),
                                               (token_no, [[P, TILES]], 1, 1), (down, [[-1, E]], E, 0)):
                pool.iota(table[:, :], pattern, base=base, channel_multiplier=step,
                          allow_small_or_imprecise_dtypes=True).then_inc(s_const, 1)

            pool.memset(minus_half[:, :], -0.5).then_inc(s_half, 1)
            pool.wait_ge(s_half, 1)
            for t in range(CHUNKS):
                pool.wait_ge(s_var, t + 1)
                pair = rstd[:, t % AHEAD, :]
                pool.tensor_tensor(pair, pair, minus_half[:, 0:CT], ALU.pow).then_inc(s_rstd, 1)

            pool.wait_ge(s_small, SMALL)
            for t in range(CHUNKS):
                pool.wait_ge(s_xn, t + 1)
                for j in range(CT):
                    k = t * CT + j
                    pool.tensor_tensor(x_sb[:, k, :], x_sb[:, k, :], b_bc[:, :], ALU.add).then_inc(s_xb, 1)

            pool.sem_inc(s_rowfree, 2)
            for c in range(CHUNKS):
                pool.wait_ge(s_var2, c + 1)
                pool.tensor_tensor(rows[:, c % 2, :, D], mv2[:, :, 1], minus_half[:, 0:CT], ALU.pow).then_inc(s_rstd2, 1)
                pool.wait_ge(s_row, c + 1)
                pool.dma_start(x2_rows[c * CT * P:(c + 1) * CT * P, :].rearrange("(t p) r -> p t r", p=P),
                               rows[:, c % 2, :, :]).then_inc(s_stored, 16)
                pool.wait_ge(s_stored, 16 * (c + 1))
                pool.sem_inc(s_rowfree, 1)

            pool.wait_ge(s_agg, CHUNKS)
            for g in got:
                pool.memset(g, 0.0).then_inc(s_clear, 1)
            pool.wait_ge(s_clear, FFN_RING)
            pool.wait_ge(s_table, 1)

            def gather(i, slot, expert):
                pool.tensor_copy(row_in[:, slot:slot + 1], slot_row[:, bass.ds(i, 1)]).then_inc(s_now, 1)
                pool.tensor_copy(score_now[:, slot:slot + 1], slot_score[:, bass.ds(i, 1)]).then_inc(s_now, 1)
                pool.tensor_copy(b1_now[:, slot, :], b1_sb[:, bass.ds(expert, 1), :].rearrange("p e j -> p (e j)")).then_inc(s_now, 1)
                pool.wait_ge(s_now, 3 * i + 3)
                pool.nop(nofuse=True)
                pool.indirect_dma_start(got[slot], None, x2_rows,
                                        bass.IndirectOffsetOnAxis(ap=row_in[:, slot:slot + 1], axis=0),
                                        bounds_check=N - 1, oob_is_err=False).then_inc(s_got[slot], 16)

            def scatter(i, k, slot):
                if not isinstance(k, int) or k >= 1:
                    pool.wait_ge(s_out[slot], 16 * k)
                pool.tensor_copy(row_out[:, slot:slot + 1], slot_row[:, bass.ds(i, 1)]).then_inc(s_pool, 1)
                pool.wait_ge(s_pool, CONSTANTS + i + 1)
                pool.wait_ge(s_done, i + 1)
                pool.nop(nofuse=True)
                pool.indirect_dma_start(out, bass.IndirectOffsetOnAxis(ap=row_out[:, slot:slot + 1], axis=0),
                                        done[slot], None, bounds_check=N - 1, oob_is_err=False).then_inc(s_out[slot], 16)

            def expert_of(i):
                return pool.value_load(expert_no[0:1, bass.ds(i, 1)], min_val=0, max_val=E - 1)

            for i in range(FFN_RING):
                gather(i, i, expert_of(i))
            for i in range(FFN_RING):
                scatter(i, 0, i)
                gather(i + FFN_RING, i, expert_of(i + FFN_RING))
            with pool.Fori(1, SLOT_TILES // FFN_RING - 1) as k:
                for u in range(FFN_RING):
                    i = k * FFN_RING + u
                    scatter(i, k, u)
                    gather(i + FFN_RING, u, expert_of(i + FFN_RING))
            for i in range(SLOT_TILES - FFN_RING, SLOT_TILES):
                scatter(i, i // FFN_RING, i % FFN_RING)
            for slot in range(FFN_RING):
                pool.wait_ge(s_out[slot], 16 * (SLOT_TILES // FFN_RING))

        @block.scalar
        def _(act):
            def copy_xnT(t, slot, transposed, copied):
                act.wait_ge(transposed, t + 1)
                nc.scalar.activation(xnT[:, slot, :, :, :], p_T[slot][:, :, :, :], ACT.Copy).then_inc(copied, 1)

            def keep_h(t, slot):
                act.wait_ge(s_H, t + 1)
                full = h_full[:, bass.ds(t * CT, CT), :]
                nc.scalar.activation(full, p_agg[slot][:, :, 0:D], ACT.Copy).then_inc(s_hi, 1)
                act.wait_ge(s_hi, 2 * t + 1)
                nc.scalar.activation(h_parts[:, bass.ds(t * CT, CT), 0, :], full, ACT.Copy).then_inc(s_hi, 1)

            copy_xnT(0, 0, s_T, s_Ts)
            with act.Fori(0, (CHUNKS - 1) // 2) as r:
                for u in range(2):
                    copy_xnT(r * 2 + (u + 1), 1 - u, s_T, s_Ts)
                    keep_h(r * 2 + u, u)
            keep_h(CHUNKS - 1, 0)

            def check(c, k, buf, slot):
                if not isinstance(c, int) or c >= 1:
                    act.wait_ge(s_chka, c)
                act.wait_ge(s_adj[buf], 16 * k)
                nc.scalar.activation(junk, adj_bits[buf][:, 0:ACT_PART, 0], ACT.Copy,
                                     accum_out=low_any[:, slot, 0:1]).then_inc(s_chka, 1)

            def low_sum(c, slot):
                act.wait_ge(s_agg, c + 1)
                act.wait_ge(s_free, c + 2)
                nc.scalar.activation(lo_sum[:, :, :], p_agg[slot][:, :, D:2 * D], ACT.Copy).then_inc(s_losum, 1)

            check(0, 1, 0, 0)
            with act.Fori(0, (CHUNKS - 1) // GNN_UNROLL) as r:
                for u in range(GNN_UNROLL):
                    c = r * GNN_UNROLL + (u + 1)
                    check(c, r * 2 + ((u + 1) // ADJ_BUFS + 1), (u + 1) % ADJ_BUFS, (u + 1) % 2)
                    low_sum(c - 1, u % 2)
                    copy_xnT(c - 1, u % 2, s_T2, s_T2s)
            low_sum(CHUNKS - 1, (CHUNKS - 1) % 2)
            copy_xnT(CHUNKS - 1, (CHUNKS - 1) % 2, s_T2, s_T2s)

            act.wait_ge(s_soft, 1)
            nc.scalar.activation(soft, soft, ACT.Exp).then_inc(s_exp, 1)

            HALF = HID // 2

            def relu_hT(i, slot):
                act.wait_ge(s_hT, i + 1)
                if not isinstance(i, int) or i >= 1:
                    act.wait_ge(s_y, i)
                act.wait_ge(s_now, 3 * i + 3)
                for j in range(HB // 2):
                    last = nc.scalar.activation(hT_sb[:, j, :], p_hT[:, j, :], ACT.Relu, bias=b1_now[:, slot, j:j + 1])
                last.then_inc(s_hTa, 1)

            def copy_h(i):
                act.wait_ge(s_h, i + 1)
                if not isinstance(i, int) or i >= 1:
                    act.wait_ge(s_hT, i)
                nc.scalar.activation(h_sb[:, 0:HALF], p_h[:, 0:HALF], ACT.Copy).then_inc(s_hsa, 1)

            def copy_fxT(i):
                act.wait_ge(s_fT, i + 1)
                if not isinstance(i, int) or i >= 1:
                    act.wait_ge(s_h, i)
                nc.scalar.activation(fxT, p_xT, ACT.Copy).then_inc(s_fTs, 1)

            copy_fxT(0)
            copy_h(0)
            copy_fxT(1)
            for i in range(FFN_RING):
                relu_hT(i, i)
                copy_h(i + 1)
                copy_fxT(i + 2)
            with act.Fori(1, SLOT_TILES // FFN_RING - 1) as k:
                for u in range(FFN_RING):
                    i = k * FFN_RING + u
                    relu_hT(i, u)
                    copy_h(i + 1)
                    copy_fxT(i + 2)
            for i in range(SLOT_TILES - FFN_RING, SLOT_TILES):
                relu_hT(i, i % FFN_RING)
                if i + 1 < SLOT_TILES:
                    copy_h(i + 1)
                if i + 2 < SLOT_TILES:
                    copy_fxT(i + 2)

        @block.tensor
        def _(pe):
            pe.wait_ge(s_wsq, 2)
            pe.wait_ge(s_ones, 1)
            for k in range(DK):
                last = nc.tensor.matmul(p_S[:, 0:D], ones[:, :], xn[:, 0, k, :], start=k == 0, stop=k == DK - 1)
            last.then_inc(s_norm, 1)

            def transpose_xn(t, slot, ready, transposed):
                pe.wait_ge(ready, t + 1)
                for j in range(CT):
                    for k in range(DK):
                        last = nc.tensor.transpose(p_T[slot][:, j, k, :], xn[:, slot, j, k * P:(k + 1) * P], ident[:, :])
                last.then_inc(transposed, 1)

            def project(t, slot):
                pe.wait_ge(s_Ts, t + 1)
                if not isinstance(t, int) or t >= 2:
                    pe.wait_ge(s_hi, 2 * t - 3)
                for j in range(CT):
                    for k in range(DK):
                        last = nc.tensor.matmul(p_agg[slot][:, j, 0:D], xnT[:, slot, j, k, :], w_sb[:, k, :],
                                                start=k == 0, stop=k == DK - 1)
                last.then_inc(s_H, 1)

            pe.wait_ge(s_const, 7)
            pe.wait_ge(s_wscaled, 1)
            transpose_xn(0, 0, s_xn, s_T)
            transpose_xn(1, 1, s_xn, s_T)
            project(0, 0)
            transpose_xn(2, 0, s_xn, s_T)
            project(1, 1)
            with pe.Fori(1, (CHUNKS - 1) // 2) as r:
                for u in range(2):
                    transpose_xn(r * 2 + (u + 1), 1 - u, s_xn, s_T)
                    project(r * 2 + u, u)
            project(CHUNKS - 1, 0)

            pe.wait_ge(s_lo, CHUNKS - 2)
            pe.wait_ge(s_hi, 2 * CHUNKS - 1)

            def aggregate(c, k_load, buf, slot, k0, k1, j):
                for k in range(k0, k1):
                    nc.tensor.matmul(p_agg[slot][:, j, :], adj_half[buf][:, k, j * P:(j + 1) * P, 1],
                                     h_parts[:, k, :, :], start=k == 0, stop=k == TILES - 1)

            def flags(c, slot):
                pe.wait_ge(s_chka, c + 1)
                pe.wait_ge(s_chkv, c + 1)
                nc.tensor.matmul(p_S[0:1, 0:2], ones[:, 0:1], low_any[:, slot, :], start=True, stop=True).then_inc(s_flag, 1)

            def learn_redo(c):
                pe.wait_ge(s_redo, c + 1)
                pe.nop(nofuse=True)
                return pe.value_load(redo[0:1, 0:1], min_val=0, max_val=1)

            def settle(again, buf, slot):
                with pe.If(again > 0):
                    for j in range(CT):
                        for k in range(TILES):
                            nc.tensor.matmul(p_agg[slot][:, j, 0:D], adj_f32[buf][:, k, j * P:(j + 1) * P],
                                             h_full[:, k, :], start=k == 0, stop=k == TILES - 1, skip_group_check=True)
                        nc.tensor.matmul(p_agg[slot][:, j, D:2 * D], zeros[:, 0:P], zeros[:, :],
                                         start=False, stop=True, skip_group_check=True)
                nc.tensor.matmul(p_S[0:1, 8:9], ones[:, 0:1], ones[:, 0:1], start=True, stop=True).then_inc(s_agg, 1)

            def router(c, slot):
                pe.wait_ge(s_T2s, c + 1)
                for j in range(CT):
                    for k in range(DK):
                        last = nc.tensor.matmul(p_log[slot][:, j, :], xnT[:, slot, j, k, :], wg_sb[:, k, :],
                                                start=k == 0, stop=k == DK - 1)
                last.then_inc(s_log, 1)

            def chunk(c, k_load, buf, slot, before):
                pe.wait_ge(s_adj[buf], 16 * k_load)
                pe.wait_ge(s_free, c + 1)
                if before:
                    aggregate(c, k_load, buf, slot, 0, FLAGS_AT, 0)
                else:
                    aggregate(c, k_load, buf, slot, 0, TILES - 2 * CT, 0)
                    pe.wait_ge(s_lo, CHUNKS)
                    pe.wait_ge(s_hi, 2 * CHUNKS)
                    aggregate(c, k_load, buf, slot, TILES - 2 * CT, TILES, 0)
                flags(c, slot)
                if before:
                    aggregate(c, k_load, buf, slot, FLAGS_AT, TILES, 0)
                aggregate(c, k_load, buf, slot, 0, TRANSPOSE_AT, 1)
                if before:
                    transpose_xn(c - 1, 1 - slot, s_xn2, s_T2)
                aggregate(c, k_load, buf, slot, TRANSPOSE_AT, ROUTER_AT, 1)
                if before:
                    router(c - 1, 1 - slot)
                again = learn_redo(c)
                aggregate(c, k_load, buf, slot, ROUTER_AT, TILES, 1)
                settle(again, buf, slot)

            chunk(0, 1, 0, 0, False)
            with pe.Fori(0, (CHUNKS - 1) // GNN_UNROLL) as r:
                for u in range(GNN_UNROLL):
                    chunk(r * GNN_UNROLL + (u + 1), r * 2 + ((u + 1) // ADJ_BUFS + 1), (u + 1) % ADJ_BUFS,
                          (u + 1) % 2, True)
            last_slot = (CHUNKS - 1) % 2
            transpose_xn(CHUNKS - 1, last_slot, s_xn2, s_T2)
            router(CHUNKS - 1, last_slot)

            pe.wait_ge(s_onehot, 1)
            pe.wait_ge(s_T2s, CHUNKS)
            nc.tensor.matmul(p_rank, earlier[:, :], onehot_f, start=True, stop=True).then_inc(s_rank, 1)
            nc.tensor.matmul(p_count, ones[:, :], onehot_f, start=True, stop=True).then_inc(s_rank, 1)
            pe.wait_ge(s_masks, 1)
            for k in range(TILES):
                last = nc.tensor.matmul(p_S[:, 0:2 * SLOT_TILES], slot_mask[:, k, :], tile_mask[:, k, :],
                                        start=k == 0, stop=k == TILES - 1)
            last.then_inc(s_slots, 1)

            def transpose_fx(i):
                pe.wait_ge(s_fx, i + 1)
                if not isinstance(i, int) or i >= 1:
                    pe.wait_ge(s_fTs, i)
                for k in range(DK):
                    last = nc.tensor.transpose(p_xT[:, k, :], fx[:, k * P:(k + 1) * P], ident[:, :])
                last.then_inc(s_fT, 1)

            def weights_at(i):
                e = pe.value_load(expert_no[0:1, bass.ds(i, 1)], min_val=0, max_val=E - 1)
                pe.wait_ge(s_w[0], 16 * (e // 2) + 16)
                pe.wait_ge(s_w[1], 16 * ((e + 1) // 2) + 16)
                return pe.snap(e * EXPERT_WORDS)

            def hidden(i, at):
                pe.wait_ge(s_fTs, i + 1)
                if not isinstance(i, int) or i >= 1:
                    pe.wait_ge(s_hsa, i)
                    pe.wait_ge(s_hsv, i)
                for n in range(HID // 512):
                    for k in range(DK):
                        last = nc.tensor.matmul(p_h[:, n * 512:(n + 1) * 512], fxT[:, k, :],
                                                arena[:, bass.ds(at + (k * HID + n * 512), 512)],
                                                start=k == 0, stop=k == DK - 1)
                last.then_inc(s_h, 1)

            def transpose_h(i):
                pe.wait_ge(s_hsa, i + 1)
                pe.wait_ge(s_hsv, i + 1)
                if not isinstance(i, int) or i >= 1:
                    pe.wait_ge(s_hTa, i)
                    pe.wait_ge(s_hTv, i)
                for j in range(HB):
                    last = nc.tensor.transpose(p_hT[:, j, :], h_sb[:, j * P:(j + 1) * P], ident[:, :])
                last.then_inc(s_hT, 1)

            def output(i, at, j0, j1):
                if j0 == 0:
                    pe.wait_ge(s_hTa, i + 1)
                    pe.wait_ge(s_hTv, i + 1)
                    if not isinstance(i, int) or i >= 1:
                        pe.wait_ge(s_yb, i)
                for j in range(j0, j1):
                    last = nc.tensor.matmul(p_y[:, 0:D], hT_sb[:, j, :],
                                            arena[:, bass.ds(at + (DK * HID + j * D), D)],
                                            start=j == 0, stop=j == HB - 1)
                if j1 == HB:
                    last.then_inc(s_y, 1)

            pe.wait_ge(s_table, 1)
            transpose_fx(0)
            hidden(0, weights_at(0))
            transpose_fx(1)

            def tile(i, has1, has2):
                transpose_h(i)
                if has1:
                    hidden(i + 1, weights_at(i + 1))
                at = weights_at(i)
                output(i, at, 0, 6)
                if has2:
                    transpose_fx(i + 2)
                output(i, at, 6, HB)

            for i in range(FFN_RING):
                tile(i, True, True)
            with pe.Fori(1, SLOT_TILES // FFN_RING - 1) as r:
                for u in range(FFN_RING):
                    tile(r * FFN_RING + u, True, True)
            for i in range(SLOT_TILES - FFN_RING, SLOT_TILES):
                tile(i, i + 1 < SLOT_TILES, i + 2 < SLOT_TILES)

        @block.vector
        def _(dve):
            chain = Chain(dve, s_dve)
            step = chain.step
            dve.wait_ge(s_wg, 16)
            for k in range(DK):
                nc.vector.tensor_tensor(xn[:, 0, k, :], w_sb[:, k, :], w_sb[:, k, :], ALU.mult).then_inc(s_wsq, 1)
            bits = lo_sum[:, 0, :].bitcast(I32)
            scale = lo_sum[:, 1, :]
            inv_bits = inv_scale[:, :].bitcast(I32)
            dve.wait_ge(s_norm, 1)
            step(nc.vector.tensor_copy(lo_sum[:, 0, :], p_S[:, 0:D]))
            step(nc.vector.tensor_scalar(bits, bits, 23, None, ALU.logical_shift_right))
            step(nc.vector.tensor_scalar(bits, bits, 1.0, None, ALU.add))
            step(nc.vector.tensor_scalar(bits, bits, 1, None, ALU.logical_shift_right))
            step(nc.vector.tensor_scalar(scale.bitcast(I32), bits, -1.0, float(SCALE_EXP), ALU.mult, ALU.add))
            step(nc.vector.tensor_scalar(scale.bitcast(I32), scale.bitcast(I32), 23, None, ALU.logical_shift_left))
            step(nc.vector.tensor_scalar(inv_bits, bits, float(INV_EXP), None, ALU.add))
            step(nc.vector.tensor_scalar(inv_bits, inv_bits, 23, None, ALU.logical_shift_left))
            nc.vector.tensor_tensor(w_sb[:, :, :], w_sb[:, :, :], scale.unsqueeze(1).to_broadcast([P, DK, D]),
                                    ALU.mult).then_inc(s_wscaled, 1)

            def row_stats(t, slot):
                for j in range(CT):
                    nc.vector.bn_stats(stats[:, slot, j, :],
                                       x_sb[:, bass.ds(t * CT + j, 1), :].rearrange("p k d -> p (k d)")).then_inc(s_stats, 1)

            def row_means(t, slot):
                dve.wait_ge(s_stats, CT * t + CT)
                dve.nop(nofuse=True)
                for j in range(CT):
                    nc.vector.bn_aggr(mv[:, slot, j, :], stats[:, slot, j, :]).then_inc(s_aggr, 1)

            def row_variances(t, slot):
                dve.wait_ge(s_aggr, CT * t + CT)
                nc.vector.tensor_scalar(rstd[:, slot, :], mv[:, slot, :, 1], EPS, None, ALU.add).then_inc(s_var, 1)

            def row_shifts(t, slot):
                dve.wait_ge(s_rstd, t + 1)
                nc.vector.scalar_tensor_tensor(out=nmr[:, slot, :], in0=mv[:, slot, :, 0], scalar=-1.0,
                                               in1=rstd[:, slot, :], op0=ALU.mult, op1=ALU.mult).then_inc(s_nmr, 1)

            def normalize(t, slot):
                dve.wait_ge(s_nmr, t + 1)
                if not isinstance(t, int) or t >= 2:
                    dve.wait_ge(s_T, t - 1)
                elif t == 0:
                    dve.wait_ge(s_norm, 1)
                for j in range(CT):
                    last = nc.vector.tensor_scalar(xn[:, slot % 2, j, :], x_sb[:, bass.ds(t * CT + j, 1), :].rearrange("p k d -> p (k d)"),
                                                   rstd[:, slot, j:j + 1], nmr[:, slot, j:j + 1], ALU.mult, ALU.add)
                last.then_inc(s_xn, 1)

            def low_part(t):
                dve.wait_ge(s_hi, 2 * t + 2)
                nc.vector.tensor_tensor(h_parts[:, bass.ds(t * CT, CT), 1, :], h_full[:, bass.ds(t * CT, CT), :],
                                        h_parts[:, bass.ds(t * CT, CT), 0, :], ALU.subtract).then_inc(s_lo, 1)

            def turn(t, slot):
                follow = CHUNKS - 1 - t if isinstance(t, int) else CHUNKS
                if follow >= 2:
                    normalize(t + 2, (slot + 2) % AHEAD)
                if follow >= AHEAD:
                    row_stats(t + AHEAD, slot)
                    row_means(t + AHEAD, slot)
                if not isinstance(t, int) or t >= 1:
                    low_part(t - 1)
                if follow >= AHEAD:
                    row_variances(t + AHEAD, slot)
                if follow >= 3:
                    row_shifts(t + 3, (slot + 3) % AHEAD)

            dve.wait_ge(s_x[0], 16)
            for t in range(AHEAD):
                row_stats(t, t)
                if t >= 2:
                    normalize(t - 2, t - 2)
                row_means(t, t)
                row_variances(t, t)
                if t >= 1:
                    row_shifts(t - 1, t - 1)
            dve.wait_ge(s_x[1], 16)
            turn(0, 0)
            with dve.Fori(0, (CHUNKS - 1 - AHEAD) // AHEAD) as r:
                for u in range(AHEAD):
                    turn(r * AHEAD + (u + 1), (u + 1) % AHEAD)
            for t in range(CHUNKS - AHEAD, CHUNKS):
                turn(t, t % AHEAD)
            low_part(CHUNKS - 1)

            def check(c, k_load, buf, slot):
                dve.wait_ge(s_adj[buf], 16 * k_load)
                nc.vector.tensor_reduce(low_any[:, slot, 1:2], adj_bits[buf][:, ACT_PART:CHUNK_WORDS, 0],
                                        AX.X, ALU.max).then_inc(s_chkv, 1)

            def decide(c):
                dve.wait_ge(s_flag, c + 1)
                nc.vector.tensor_reduce(low_top[:, :], p_S[0:1, 0:2], AX.X, ALU.max).then_inc(s_lowtop, 1)
                dve.wait_ge(s_lowtop, c + 1)
                nc.vector.tensor_scalar(redo[:, :], low_top[:, :], 0.0, None, ALU.is_gt).then_inc(s_redo, 1)

            STEPS = 2 + 2 * CT
            finish_base = chain.n

            def finish(c, slot):
                chain.enter(c * STEPS + finish_base)
                r = rows[:, slot, :, 0:D]
                dve.wait_ge(s_losum, c + 1)
                dve.wait_ge(s_rowfree, c + 1)
                nc.vector.tensor_tensor(r, p_agg[slot][:, :, 0:D], lo_sum[:, :, :], ALU.add).then_inc(s_free, 1)
                dve.wait_ge(s_free, c + 3)
                step(nc.vector.tensor_tensor(r, r, inv_scale[:, :].unsqueeze(1).to_broadcast([P, CT, D]), ALU.mult))
                dve.wait_ge(s_xb, CT * c + CT)
                step(nc.vector.tensor_tensor(r, r, x_sb[:, bass.ds(c * CT, CT), :], ALU.add))
                for j in range(CT):
                    chain.mark(nc.vector.bn_stats(stats2[:, j, :], rows[:, slot, j, 0:D]))
                chain.wait()
                dve.nop(nofuse=True)
                for j in range(CT):
                    chain.mark(nc.vector.bn_aggr(mv2[:, j, :], stats2[:, j, :]))
                chain.wait()
                nc.vector.tensor_scalar(mv2[:, :, 1], mv2[:, :, 1], EPS, None, ALU.add).then_inc(s_var2, 1)
                dve.wait_ge(s_rstd2, c + 1)
                nc.vector.scalar_tensor_tensor(out=rows[:, slot, :, D + 1], in0=mv2[:, :, 0], scalar=-1.0,
                                               in1=rows[:, slot, :, D], op0=ALU.mult, op1=ALU.mult).then_inc(s_row, 1)
                dve.wait_ge(s_row, c + 1)
                for j in range(CT):
                    last = nc.vector.tensor_scalar(xn[:, slot, j, :], rows[:, slot, j, 0:D], rows[:, slot, j, D:D + 1],
                                                   rows[:, slot, j, D + 1:D + 2], ALU.mult, ALU.add)
                last.then_inc(s_xn2, 1)

            def keep_logits(c, slot):
                dve.wait_ge(s_log, c + 1)
                nc.vector.tensor_tensor(logits[:, bass.ds(c * CT, CT), :], p_log[slot], bg_sb[:, :, :],
                                        ALU.add).then_inc(s_logs, 1)

            dve.wait_ge(s_lo, CHUNKS)
            dve.sem_inc(s_free, 2)
            dve.wait_ge(s_small, SMALL)
            check(0, 1, 0, 0)
            decide(0)
            with dve.Fori(0, (CHUNKS - 1) // GNN_UNROLL) as r:
                for u in range(GNN_UNROLL):
                    c = r * GNN_UNROLL + (u + 1)
                    check(c, r * 2 + ((u + 1) // ADJ_BUFS + 1), (u + 1) % ADJ_BUFS, (u + 1) % 2)
                    decide(c)
                    finish(c - 1, u % 2)
                    keep_logits(c - 1, u % 2)
            finish(CHUNKS - 1, (CHUNKS - 1) % 2)
            keep_logits(CHUNKS - 1, (CHUNKS - 1) % 2)
            chain.enter(finish_base + CHUNKS * STEPS)
            dve.wait_ge(s_logs, CHUNKS)

            def over_experts(a):
                return a.unsqueeze(2).to_broadcast([P, TILES, E])

            step(nc.vector.tensor_reduce(top, logits[:, :, :], AX.X, ALU.max))
            nc.vector.tensor_tensor(soft, logits[:, :, :], over_experts(top), ALU.subtract).then_inc(s_soft, 1)
            step(nc.vector.tensor_tensor(pick, logits[:, :, :], over_experts(top), ALU.is_equal))
            step(nc.vector.tensor_tensor(pick, pick, down[:, :].unsqueeze(1).to_broadcast([P, TILES, E]), ALU.mult))
            step(nc.vector.tensor_reduce(first, pick, AX.X, ALU.max))
            step(nc.vector.tensor_scalar(is_token[:, :], padding[:, :], -1.0, 1.0, ALU.mult, ALU.add))
            step(nc.vector.tensor_tensor(pick, pick, over_experts(first), ALU.is_equal))
            nc.vector.tensor_tensor(onehot, pick.rearrange("p k e -> p e k"),
                                    is_token[:, :].unsqueeze(1).to_broadcast([P, E, TILES]), ALU.mult).then_inc(s_onehot, 1)
            step(nc.vector.memset(ones_w, 1.0))
            step(nc.vector.memset(running[:, 0:1], 0.0))
            dve.wait_ge(s_exp, 1)
            step(nc.vector.tensor_reduce(score, soft, AX.X, ALU.add))
            step(nc.vector.reciprocal(score, score))
            dve.wait_ge(s_rank, 2)
            step(nc.vector.tensor_tensor_scan(running[:, 1:1 + E * TILES], ones_w, p_count, 0.0, ALU.mult, ALU.add))
            run_start = running[:, 0:E * TILES].rearrange("p (e k) -> p e k", e=E)
            run_end = running[:, 1:1 + E * TILES].rearrange("p (e k) -> p e k", e=E)
            step(nc.vector.tensor_tensor(tiles_f, run_end[:, :, TILES - 1], run_start[:, :, 0], ALU.subtract))
            step(nc.vector.tensor_scalar(tiles_i, tiles_f, float(P - 1), None, ALU.add))
            step(nc.vector.tensor_scalar(tiles_i, tiles_i, P.bit_length() - 1, None, ALU.logical_shift_right))
            step(nc.vector.tensor_copy(tiles_f, tiles_i))
            step(nc.vector.tensor_tensor_scan(tile_end, ones_w[:, 0:E], tiles_f, 0.0, ALU.mult, ALU.add))
            step(nc.vector.tensor_tensor(start_e, tile_end, tiles_f, ALU.subtract))
            step(nc.vector.scalar_tensor_tensor(out=start_e, in0=start_e, scalar=float(P), in1=run_start[:, :, 0],
                                                op0=ALU.mult, op1=ALU.subtract))
            step(nc.vector.tensor_tensor(slot_no, run_start, start_e.unsqueeze(2).to_broadcast([P, E, TILES]), ALU.add))
            step(nc.vector.tensor_tensor(slot_no, slot_no, p_rank.rearrange("p (e k) -> p e k", e=E), ALU.add))
            step(nc.vector.tensor_tensor(slot_no, slot_no, onehot, ALU.mult))
            step(nc.vector.tensor_reduce(pos, slot_no.rearrange("p e k -> p k e"), AX.X, ALU.add))
            step(nc.vector.scalar_tensor_tensor(out=pos, in0=padding[:, :], scalar=float(SLOT_TILES * P), in1=pos,
                                                op0=ALU.mult, op1=ALU.add))
            step(nc.vector.tensor_copy(pos_i[:, 2, :], pos))
            step(nc.vector.tensor_scalar(pos_i[:, 0, :], pos_i[:, 2, :], P.bit_length() - 1, None, ALU.logical_shift_right))
            step(nc.vector.tensor_scalar(pos_i[:, 1, :], pos_i[:, 2, :], P - 1, None, ALU.bitwise_and))
            step(nc.vector.tensor_copy(pos_f, pos_i[:, 0:2, :]))
            def over(a, n):
                return a.unsqueeze(2).to_broadcast([P, TILES, n])

            in_tile, scored = tile_mask[:, :, 0:SLOT_TILES], tile_mask[:, :, SLOT_TILES:2 * SLOT_TILES]
            step(nc.vector.tensor_tensor(slot_mask, iota_slot[:, :].unsqueeze(1).to_broadcast([P, TILES, P]),
                                         over(pos_f[:, 1, :], P), ALU.is_equal))
            step(nc.vector.tensor_tensor(in_tile, iota_tile[:, :].unsqueeze(1).to_broadcast([P, TILES, SLOT_TILES]),
                                         over(pos_f[:, 0, :], SLOT_TILES), ALU.is_equal))
            step(nc.vector.tensor_tensor(scored, in_tile, over(score, SLOT_TILES), ALU.mult))
            nc.vector.tensor_tensor(in_tile, in_tile, over(token_no[:, :], SLOT_TILES), ALU.mult).then_inc(s_masks, 1)
            step(nc.vector.tensor_tensor(ended, iota_tile[0:1, :].unsqueeze(2).to_broadcast([1, SLOT_TILES, E]),
                                         tile_end[0:1, :].unsqueeze(1).to_broadcast([1, SLOT_TILES, E]), ALU.is_ge))
            step(nc.vector.tensor_reduce(expert_f, ended, AX.X, ALU.add))
            step(nc.vector.tensor_scalar(expert_no[:, :], expert_f, float(E - 1), None, ALU.min))
            dve.wait_ge(s_slots, 1)
            step(nc.vector.tensor_copy(slot_score[:, :], p_S[:, SLOT_TILES:2 * SLOT_TILES]))
            step(nc.vector.tensor_scalar(row_f, p_S[:, 0:SLOT_TILES], 1.0, SKIP, ALU.is_lt, ALU.mult))
            nc.vector.scalar_tensor_tensor(out=slot_row[:, :], in0=p_S[:, 0:SLOT_TILES], scalar=-1.0, in1=row_f,
                                           op0=ALU.add, op1=ALU.add).then_inc(s_table, 1)
            dve.wait_ge(s_table, 1)
            dve.wait_ge(s_w[1], 16)

            HALF = HID // 2

            def relu_hT(i, slot):
                dve.wait_ge(s_hT, i + 1)
                if not isinstance(i, int) or i >= 1:
                    dve.wait_ge(s_y, i)
                dve.wait_ge(s_now, 3 * i + 3)
                for j in range(HB // 2, HB):
                    last = nc.vector.tensor_scalar(hT_sb[:, j, :], p_hT[:, j, :], b1_now[:, slot, j:j + 1], 0.0,
                                                   ALU.add, ALU.max)
                last.then_inc(s_hTv, 1)

            def copy_h(i):
                dve.wait_ge(s_h, i + 1)
                if not isinstance(i, int) or i >= 1:
                    dve.wait_ge(s_hT, i)
                nc.vector.tensor_copy(h_sb[:, HALF:HID], p_h[:, HALF:HID]).then_inc(s_hsv, 1)

            def normalize_rows(i, k, slot):
                dve.wait_ge(s_got[slot], 16 * k + 16)
                if not isinstance(i, int) or i >= 1:
                    dve.wait_ge(s_fT, i)
                g = got[slot]
                nc.vector.tensor_scalar(fx, g[:, 0:D], g[:, D:D + 1], g[:, D + 1:D + 2], ALU.mult, ALU.add).then_inc(s_fx, 1)

            def finish_rows(i, k, slot):
                e = dve.value_load(expert_no[0:1, bass.ds(i, 1)], min_val=0, max_val=E - 1)
                dve.wait_ge(s_y, i + 1)
                nc.vector.tensor_tensor(yb, p_y[:, 0:D], b2_sb[:, bass.ds(e, 1), :].rearrange("p e d -> p (e d)"),
                                        ALU.add).then_inc(s_yb, 1)
                dve.wait_ge(s_yb, i + 1)
                if not isinstance(k, int) or k >= 1:
                    dve.wait_ge(s_out[slot], 16 * k)
                nc.vector.scalar_tensor_tensor(out=done[slot], in0=yb, scalar=score_now[:, slot:slot + 1],
                                               in1=got[slot][:, 0:D], op0=ALU.mult, op1=ALU.add).then_inc(s_done, 1)

            normalize_rows(0, 0, 0)
            copy_h(0)
            normalize_rows(1, 0, 1)
            for i in range(FFN_RING):
                relu_hT(i, i)
                copy_h(i + 1)
                normalize_rows(i + 2, (i + 2) // FFN_RING, (i + 2) % FFN_RING)
                finish_rows(i, 0, i)
            with dve.Fori(1, SLOT_TILES // FFN_RING - 1) as k:
                for u in range(FFN_RING):
                    i = k * FFN_RING + u
                    relu_hT(i, u)
                    copy_h(i + 1)
                    normalize_rows(i + 2, k + (u + 2) // FFN_RING, (u + 2) % FFN_RING)
                    finish_rows(i, k, u)
            for i in range(SLOT_TILES - FFN_RING, SLOT_TILES):
                relu_hT(i, i % FFN_RING)
                if i + 1 < SLOT_TILES:
                    copy_h(i + 1)
                if i + 2 < SLOT_TILES:
                    normalize_rows(i + 2, (i + 2) // FFN_RING, (i + 2) % FFN_RING)
                finish_rows(i, i // FFN_RING, i % FFN_RING)


def kernel(x, adj, L0_gnn_W, L0_gnn_b, L0_ffn_Wg, L0_ffn_bg, L0_ffn_W1, L0_ffn_b1, L0_ffn_W2, L0_ffn_b2):
    import numpy as np
    import concourse.bacc as bacc
    from concourse.bass_utils import run_bass_kernel_spmd

    x, adj = np.asarray(x), np.asarray(adj)
    x_pad = np.zeros((NPAD, D), x.dtype)
    x_pad[:N] = x
    adj_t = np.zeros((NPAD, NPAD), adj.dtype)
    adj_t[:N, :N] = adj.T
    w1, w2 = np.asarray(L0_ffn_W1), np.asarray(L0_ffn_W2)
    arrays = {
        "x": x_pad.reshape(TILES, P, D).transpose(1, 0, 2),
        "adj": adj_t.reshape(TILES, P, CHUNKS, CT * P).transpose(2, 1, 0, 3).reshape(CHUNKS, P, CHUNK_WORDS),
        "w_gnn": np.asarray(L0_gnn_W).transpose(1, 0, 2).reshape(DK, P, D).transpose(1, 0, 2),
        "b_gnn": np.asarray(L0_gnn_b).reshape(1, D),
        "w_gate": np.asarray(L0_ffn_Wg).reshape(DK, P, E).transpose(1, 0, 2),
        "b_gate": np.asarray(L0_ffn_bg).reshape(1, E),
        "w_exp": np.concatenate([w1.reshape(E, DK, P, HID).transpose(0, 2, 1, 3).reshape(E, P, DK * HID),
                                 w2.reshape(E, HB, P, D).transpose(0, 2, 1, 3).reshape(E, P, HB * D)], axis=2),
        "b1": np.asarray(L0_ffn_b1).reshape(E, HB, P).transpose(2, 0, 1),
        "b2": np.asarray(L0_ffn_b2).reshape(1, E * D),
    }
    arrays = {name: np.ascontiguousarray(a) for name, a in arrays.items()}
    nc = bacc.Bacc("TRN2", target_bir_lowering=False, num_devices=1)
    args = [nc.dram_tensor(name, a.shape, mybir.dt.from_np(a.dtype), kind="ExternalInput").ap()
            for name, a in arrays.items()]
    out = nc.dram_tensor("out", (N, D), F32, kind="ExternalOutput").ap()
    build(nc, *args, out)
    r = run_bass_kernel_spmd(nc, [arrays], core_ids=[0])
    return r.results[0]["out"]
```

```python
from contextlib import ExitStack

import concourse.bass as bass
from concourse import mybir

ALU = mybir.AluOpType
ACT = mybir.ActivationFunctionType
AX = mybir.AxisListType
F32 = mybir.dt.float32
F16 = mybir.dt.float16
BF16 = mybir.dt.bfloat16
U16 = mybir.dt.uint16
I32 = mybir.dt.int32

P = 128
N = 3327
D = 256
DK = D // P
TILES = -(-N // P)
NPAD = TILES * P
CT = 2
CHUNKS = TILES // CT
CHUNK_WORDS = TILES * CT * P
E = 8
HID = 1024
HB = HID // P
SLOT_TILES = (N + E * (P - 1)) // P
ROW = D + 4
EPS = 1e-5
ADJ_BUFS = 3
GNN_UNROLL = 2 * ADJ_BUFS
AHEAD = 4
FIRST_TILES = AHEAD * CT
FFN_RING = 3
EXPERT_WORDS = DK * HID + HB * D
EARLY = 1
FLAGS_AT = 8
TRANSPOSE_AT = 10
ROUTER_AT = 16
ACT_PART = 4096
WARM_START, WARM_PROJECT, WARM_ROUTER, WARM_RANKS, WARM_TABLE, WARM_TABLE_2, WARM_FFN = 9, 9, 24, 10, 46, 12, 23
VALUES = 5
MASK_PARTS = 2
SKIP = 100000.0
SCALE_EXP = 201
INV_EXP = 254 - SCALE_EXP

assert (CHUNKS - 1) % GNN_UNROLL == 0 and SLOT_TILES % FFN_RING == 0


class Chain:

    def __init__(self, eng, sem):
        self.eng, self.sem, self.base, self.n = eng, sem, 0, 0

    def enter(self, base):
        self.base, self.n = base, 0

    def mark(self, ins):
        self.n += 1
        ins.then_inc(self.sem, 1)

    def wait(self):
        self.eng.wait_ge(self.sem, self.base + self.n)

    def step(self, ins):
        self.mark(ins)
        self.wait()


def build(nc, x, adj, w_gnn, b_gnn, w_gate, b_gate, w_exp, b1, b2, out):
    with ExitStack() as ctx:
        def sb(name, shape, dt=F32):
            return ctx.enter_context(nc.sbuf_tensor(name, shape, dt))

        def ps(name, shape):
            return ctx.enter_context(nc.psum_tensor(name, shape, F32))

        def sem(name):
            return ctx.enter_context(nc.semaphore(name))

        x2_rows = nc.dram_tensor("x2_rows", (NPAD, ROW), F32, kind="Internal").ap()

        ADJ0 = EARLY * EXPERT_WORDS
        HP0 = ADJ0 + ADJ_BUFS * CHUNK_WORDS
        arena = sb("arena", [P, max(HP0 + TILES * D + ACT_PART // 2, E * EXPERT_WORDS)])
        adj_sb = [arena[:, ADJ0 + s * CHUNK_WORDS:ADJ0 + (s + 1) * CHUNK_WORDS] for s in range(ADJ_BUFS)]
        adj_f32 = [a.rearrange("p (k n) -> p k n", n=CT * P) for a in adj_sb]
        adj_half = [a.bitcast(BF16).rearrange("p (k n two) -> p k n two", n=CT * P, two=2) for a in adj_sb]
        adj_bits = [a.bitcast(U16).rearrange("p (w two) -> p w two", two=2) for a in adj_sb]
        junk = arena[:, HP0 + TILES * D:HP0 + TILES * D + ACT_PART // 2].bitcast(BF16)
        h_parts = arena[:, HP0:HP0 + TILES * D].bitcast(F16).rearrange("p (k s d) -> p k s d", s=2, d=D)
        x_sb = sb("x_sb", [P, TILES, D])
        reuse = sb("reuse", [P, TILES * D])
        h_full = reuse[:, :].rearrange("p (k d) -> p k d", d=D)

        ident = sb("ident", [P, P])
        ones = sb("ones", [P, P])
        zeros = sb("zeros", [P, D])
        earlier = sb("earlier", [P, P])
        w_sb = sb("w_sb", [P, DK, D])
        wg_sb = sb("wg_sb", [P, DK, E])
        bg_sb = sb("bg_sb", [P, CT, E])
        b1_sb = sb("b1_sb", [P, E, HB])
        b_bc = sb("b_bc", [P, D])
        inv_scale = sb("inv_scale", [P, D])
        stats = sb("stats", [P, AHEAD, CT, 6])
        mv = sb("mv", [P, AHEAD, CT, 2])
        rstd = sb("rstd", [P, AHEAD, CT])
        nmr = sb("nmr", [P, AHEAD, CT])
        xn = sb("xn", [P, 2, CT, D])
        xnT = sb("xnT", [P, 2, CT, DK, P])
        rows = sb("rows", [P, 2, CT, ROW])
        lo_sum = sb("lo_sum", [P, CT, D])
        stats2 = sb("stats2", [P, CT, 6])
        mv2 = sb("mv2", [P, CT, 2])
        minus_half = sb("minus_half", [P, TILES])
        logits = sb("logits", [P, TILES, E])
        low_any = sb("low_any", [P, 2, 2])
        low_top = sb("low_top", [1, 1])
        redo = sb("redo", [1, 1], I32)

        iota_tile = sb("iota_tile", [P, SLOT_TILES])
        iota_tile_b = sb("iota_tile_b", [P, SLOT_TILES], BF16)
        iota_slot_b = sb("iota_slot_b", [P, P], BF16)
        values = sb("values", [P, TILES, VALUES], BF16)
        scan_ones = sb("scan_ones", [P, E * TILES])
        padding = sb("padding", [P, TILES])
        is_token = sb("is_token", [P, TILES])
        down = sb("down", [P, E])
        slot_row = sb("slot_row", [P, SLOT_TILES], I32)
        slot_score = sb("slot_score", [P, SLOT_TILES])
        expert_no = sb("expert_no", [1, SLOT_TILES], I32)
        tiles_used = sb("tiles_used", [1, 1], I32)
        row_in = sb("row_in", [P, FFN_RING], I32)
        row_out = sb("row_out", [P, FFN_RING], I32)
        score_now = sb("score_now", [P, FFN_RING])
        b1_now = sb("b1_now", [P, FFN_RING, HB])

        class Cut:
            def __init__(self, ap, size):
                self.ap, self.at, self.size = ap, 0, size

            def take(self, n):
                self.at += n
                assert self.at <= self.size
                return self.ap[:, self.at - n:self.at]

        cut = Cut(x_sb[:, :, :].rearrange("p k d -> p (k d)"), TILES * D)
        slot_mask = cut.take(TILES * P // 2).bitcast(BF16).rearrange("p (k s) -> p k s", s=P)
        in_tile = cut.take(TILES * SLOT_TILES // 2).bitcast(BF16).rearrange("p (k i) -> p k i", i=SLOT_TILES)
        tile_mask = cut.take(TILES * VALUES * SLOT_TILES // 2).bitcast(BF16).rearrange(
            "p (k v i) -> p k v i", v=VALUES, i=SLOT_TILES)
        table = cut.take(VALUES * SLOT_TILES).rearrange("p (v i) -> p v i", i=SLOT_TILES)
        rest = cut.take(TILES)
        soft = cut.take(TILES * E).rearrange("p (k e) -> p k e", e=E)
        pick = cut.take(TILES * E).rearrange("p (k e) -> p k e", e=E)
        onehot_f = cut.take(E * TILES)
        onehot = onehot_f.rearrange("p (e k) -> p e k", e=E)
        slot_no = cut.take(E * TILES).rearrange("p (e k) -> p e k", e=E)
        top = cut.take(TILES)
        first = cut.take(TILES)
        score = cut.take(TILES)
        running = cut.take(1 + E * TILES)
        tiles_i = cut.take(E).bitcast(I32)
        tiles_f = cut.take(E)
        tile_end = cut.take(E)
        start_e = cut.take(E)
        pos = cut.take(TILES)
        pos_i = cut.take(3 * TILES).bitcast(I32).rearrange("p (w k) -> p w k", w=3)
        pos_b = cut.take(TILES).bitcast(BF16).rearrange("p (w k) -> p w k", w=2)
        cut = Cut(xnT[:, :, :, :, :].rearrange("p s c k t -> p (s c k t)"), 2 * CT * D)
        ended = cut.take(SLOT_TILES * E)[0:1, :].rearrange("p (i e) -> p i e", e=E)
        expert_f = cut.take(SLOT_TILES)[0:1, :]
        row_f = cut.take(SLOT_TILES)

        cut2 = Cut(reuse, TILES * D)
        b2_sb = cut2.take(E * D).rearrange("p (e d) -> p e d", d=D)
        h_sb = cut2.take(HID)
        hT_sb = cut2.take(HID).rearrange("p (j t) -> p j t", t=P)
        got = [cut2.take(ROW) for _ in range(FFN_RING)]
        done = [cut2.take(D) for _ in range(FFN_RING)]
        fx = cut2.take(D)
        fxT = cut2.take(D).rearrange("p (k t) -> p k t", t=P)
        yb = cut2.take(D)

        p_agg = [ps(f"p_agg{s}", [P, CT, 512]) for s in range(2)]
        p_T = [ps(f"p_T{s}", [P, CT, DK, P]) for s in range(2)]
        p_S = ps("p_S", [P, 512])
        p_y = ps("p_y", [P, 512])
        p_log = [p_y[:, s * 64:s * 64 + CT * E].rearrange("p (c e) -> p c e", e=E) for s in range(2)]
        p_h = p_agg[0][:, :, :].rearrange("p c n -> p (c n)")
        p_hT = p_agg[1][:, :, :].rearrange("p c (j t) -> p (c j) t", t=P)
        p_xT = p_T[0][:, 0, :, :]
        p_rank, p_count = (t[:, :, :, :].rearrange("p c k t -> p (c k t)")[:, 0:E * TILES] for t in p_T)

        s_x = [sem(f"x_loaded{i}") for i in range(2)]
        s_wg = sem("w_gnn_loaded")
        s_small = sem("small_loaded")
        s_adj = [sem(f"adj_loaded{i}") for i in range(ADJ_BUFS)]
        s_w = [sem(f"weights_loaded{i}") for i in range(2)]
        s_const = sem("constants_made")
        s_pool = sem("pool_chain")
        s_dve = sem("dve_chain")
        s_wsq = sem("w_squared")
        s_norm = sem("column_norms_summed")
        s_wscaled = sem("w_scaled")
        s_ones = sem("ones_made")
        s_stats = sem("statistics_of_half_rows_ready")
        s_aggr = sem("means_and_variances_ready")
        s_var = sem("variances_ready")
        s_half = sem("minus_half_made")
        s_rstd = sem("rstds_ready")
        s_nmr = sem("means_times_rstds_ready")
        s_xn = sem("xn_ready")
        s_T = sem("xn_transposed")
        s_Ts = sem("xnT_in_sbuf")
        s_H = sem("h_summed")
        s_hi = sem("h_high_and_full_copied")
        s_lo = sem("h_low_copied")
        s_xb = sem("b_added_to_x")
        s_chkv = sem("low_halves_checked_dve")
        s_chka = sem("low_halves_checked_act")
        s_flag = sem("flags_summed")
        s_lowtop = sem("flags_reduced")
        s_redo = sem("redo_known")
        s_agg = sem("chunk_aggregated")
        s_losum = sem("low_sum_copied")
        s_free = sem("aggregate_read")
        s_var2 = sem("var2_ready")
        s_rstd2 = sem("rstd2_ready")
        s_xn2 = sem("xn2_ready")
        s_row = sem("rows_ready")
        s_stored = sem("rows_stored")
        s_rowfree = sem("row_slot_free")
        s_T2 = sem("xn2_transposed")
        s_T2s = sem("xn2T_in_sbuf")
        s_log = sem("logits_summed")
        s_logs = sem("logits_in_sbuf")
        s_soft = sem("softmax_argument_ready")
        s_exp = sem("exp_ready")
        s_onehot = sem("onehot_ready")
        s_rank = sem("ranks_summed")
        s_masks = sem("masks_ready")
        s_slots = sem("slots_summed")
        s_table = sem("tables_ready")
        s_clear = sem("gather_buffers_cleared")
        s_got = [sem(f"rows_gathered{i}") for i in range(FFN_RING)]
        s_rownow = sem("tile_row_numbers_copied")
        s_now = sem("tile_columns_copied")
        s_fx = sem("ffn_xn_ready")
        s_fT = sem("ffn_xn_transposed")
        s_fTs = sem("ffn_xnT_in_sbuf")
        s_h = sem("hidden_summed")
        s_hsa = sem("hidden_copied_act")
        s_hsv = sem("hidden_copied_dve")
        s_hT = sem("hidden_transposed")
        s_hTa = sem("hiddenT_relu_act")
        s_hTv = sem("hiddenT_relu_dve")
        s_y = sem("ffn_summed")
        s_yb = sem("ffn_sum_read")
        s_done = sem("rows_finished")
        s_out = [sem(f"rows_scattered{i}") for i in range(FFN_RING)]
        SMALL = 16 * 4

        def used_tiles(eng):
            return eng.value_load(tiles_used[0:1, 0:1], min_val=TILES, max_val=SLOT_TILES)

        block = ctx.enter_context(nc.Block())

        @block.sync
        def _(sp):
            sp.dma_start(w_sb[:, :, :], w_gnn).then_inc(s_wg, 16)
            for i, (k0, k1) in enumerate(((0, FIRST_TILES), (FIRST_TILES, TILES))):
                sp.dma_start(x_sb[:, k0:k1, :], x[:, k0:k1, :]).then_inc(s_x[i], 16)
            for c in range(ADJ_BUFS):
                sp.dma_start(adj_sb[c], adj[c]).then_inc(s_adj[c], 16)

            def load_expert(e):
                if e >= 1:
                    sp.wait_ge(s_w[e % 2], 16 * ((e + 1) // 2))
                sp.dma_start(arena[:, e * EXPERT_WORDS:(e + 1) * EXPERT_WORDS], w_exp[e]).then_inc(s_w[e % 2], 16)

            def reload(c, buf):
                sp.wait_ge(s_agg, c - (ADJ_BUFS - 1))
                sp.dma_start(adj_sb[buf], adj[bass.ds(c, 1), :, :].rearrange("c p w -> p (c w)")).then_inc(s_adj[buf], 16)

            turns = (CHUNKS - ADJ_BUFS) // ADJ_BUFS
            with sp.Fori(0, turns) as r:
                for u in range(ADJ_BUFS):
                    reload(r * ADJ_BUFS + (ADJ_BUFS + u), u)
            for c in range(ADJ_BUFS + turns * ADJ_BUFS, CHUNKS):
                reload(c, c % ADJ_BUFS)
            for e in range(EARLY):
                load_expert(e)
            sp.wait_ge(s_agg, CHUNKS)
            sp.dma_start(b2_sb.rearrange("p e d -> p (e d)"), b2.to_broadcast([P, E * D])).then_inc(s_w[1], 16)
            for e in range(EARLY, E):
                if e == E - 3:
                    sp.wait_ge(s_got[FFN_RING - 1], 16)
                if e > E - 3:
                    sp.wait_ge(s_w[(e - 1) % 2], 16 * (e // 2 + 1))
                load_expert(e)

        @block.gpsimd
        def _(pool):
            pool.memset(ones[:, :], 1.0).then_inc(s_ones, 1)
            pool.dma_start(wg_sb[:, :, :], w_gate).then_inc(s_small, 16)
            pool.dma_start(bg_sb[:, :, :], b_gate.unsqueeze(0).to_broadcast([P, CT, E])).then_inc(s_small, 16)
            pool.dma_start(b1_sb[:, :, :], b1).then_inc(s_small, 16)
            pool.dma_start(b_bc[:, :], b_gnn.to_broadcast([P, D])).then_inc(s_small, 16)
            chain = Chain(pool, s_pool)
            chain.mark(pool.memset(ident[:, :], 0.0))
            chain.mark(pool.memset(zeros[:, :], 0.0))
            chain.mark(pool.memset(padding[:, :], 0.0))
            chain.mark(pool.memset(rows[:, :, :, D:ROW], 0.0))
            chain.wait()
            CONSTANTS = chain.n
            pool.wait_ge(s_ones, 1)
            pool.affine_select(out=ident[:, :], in_=ident[:, :], compare_op=ALU.not_equal, fill=1.0,
                               base=0, pattern=[[-1, P]], channel_multiplier=1).then_inc(s_const, 1)
            pool.affine_select(out=earlier[:, :], in_=ones[:, :], compare_op=ALU.is_gt, fill=0.0,
                               base=0, pattern=[[1, P]], channel_multiplier=-1).then_inc(s_const, 1)
            pool.affine_select(out=padding[:, :], in_=padding[:, :], compare_op=ALU.is_gt, fill=1.0,
                               base=N, pattern=[[-P, TILES]], channel_multiplier=-1).then_inc(s_const, 1)
            for index, pattern, base, step in (
                    (iota_tile[:, :], [[1, SLOT_TILES]], 0, 0), (iota_tile_b[:, :], [[1, SLOT_TILES]], 0, 0),
                    (iota_slot_b[:, :], [[1, P]], 0, 0), (values[:, :, 0], [[1, TILES]], 0, 0),
                    (values[:, :, 1], [[0, TILES]], 1, 1), (down[:, :], [[-1, E]], E, 0)):
                pool.iota(index, pattern, base=base, channel_multiplier=step,
                          allow_small_or_imprecise_dtypes=True).then_inc(s_const, 1)

            pool.memset(minus_half[:, :], -0.5).then_inc(s_half, 1)
            pool.wait_ge(s_half, 1)
            def row_rstds(t):
                pool.wait_ge(s_var, t + 1)
                pair = rstd[:, t % AHEAD, :]
                pool.tensor_tensor(pair, pair, minus_half[:, 0:CT], ALU.pow).then_inc(s_rstd, 1)

            def low_part(t):
                pool.wait_ge(s_hi, 2 * t + 2)
                pool.tensor_tensor(h_parts[:, t * CT:(t + 1) * CT, 1, :], h_full[:, t * CT:(t + 1) * CT, :],
                                   h_parts[:, t * CT:(t + 1) * CT, 0, :], ALU.subtract).then_inc(s_lo, 1)

            for t in range(AHEAD):
                row_rstds(t)
            for t in range(CHUNKS):
                if t + AHEAD < CHUNKS:
                    row_rstds(t + AHEAD)
                if t >= 1:
                    low_part(t - 1)
            low_part(CHUNKS - 1)

            def add_b(t):
                pool.wait_ge(s_xn, t + 1)
                for k in range(t * CT, (t + 1) * CT):
                    pool.tensor_tensor(x_sb[:, k, :], x_sb[:, k, :], b_bc[:, :], ALU.add).then_inc(s_xb, 1)

            pool.wait_ge(s_small, SMALL)
            B_AHEAD = 5
            for t in range(B_AHEAD):
                add_b(t)

            pool.sem_inc(s_rowfree, 2)
            for c in range(CHUNKS):
                pool.wait_ge(s_var2, c + 1)
                pool.tensor_tensor(rows[:, c % 2, :, D], mv2[:, :, 1], minus_half[:, 0:CT], ALU.pow).then_inc(s_rstd2, 1)
                pool.wait_ge(s_row, c + 1)
                pool.dma_start(x2_rows[c * CT * P:(c + 1) * CT * P, :].rearrange("(t p) r -> p t r", p=P),
                               rows[:, c % 2, :, :]).then_inc(s_stored, 16)
                if c + B_AHEAD < CHUNKS:
                    add_b(c + B_AHEAD)
                pool.wait_ge(s_stored, 16 * (c + 1))
                pool.sem_inc(s_rowfree, 1)

            pool.wait_ge(s_agg, CHUNKS)
            for g in got:
                pool.memset(g, 0.0).then_inc(s_clear, 1)
            pool.wait_ge(s_clear, FFN_RING)
            pool.wait_ge(s_table, 1)

            def gather(i, slot):
                pool.tensor_copy(row_in[:, slot:slot + 1], slot_row[:, bass.ds(i, 1)]).then_inc(s_rownow, 1)
                pool.wait_ge(s_rownow, i + 1)
                pool.nop(nofuse=True)
                pool.indirect_dma_start(got[slot], None, x2_rows,
                                        bass.IndirectOffsetOnAxis(ap=row_in[:, slot:slot + 1], axis=0),
                                        bounds_check=N - 1, oob_is_err=False).then_inc(s_got[slot], 16)

            def pick_columns(i, slot):
                expert = pool.value_load(expert_no[0:1, bass.ds(i, 1)], min_val=0, max_val=E - 1)
                pool.tensor_copy(score_now[:, slot:slot + 1], slot_score[:, bass.ds(i, 1)]).then_inc(s_now, 1)
                pool.tensor_copy(b1_now[:, slot, :], b1_sb[:, bass.ds(expert, 1), :].rearrange("p e j -> p (e j)")).then_inc(s_now, 1)

            def scatter(i, k, slot):
                if not isinstance(k, int) or k >= 1:
                    pool.wait_ge(s_out[slot], 16 * k)
                pool.tensor_copy(row_out[:, slot:slot + 1], slot_row[:, bass.ds(i, 1)]).then_inc(s_pool, 1)
                pool.wait_ge(s_pool, CONSTANTS + i + 1)
                pool.wait_ge(s_done, i + 1)
                pool.nop(nofuse=True)
                pool.indirect_dma_start(out, bass.IndirectOffsetOnAxis(ap=row_out[:, slot:slot + 1], axis=0),
                                        done[slot], None, bounds_check=N - 1, oob_is_err=False).then_inc(s_out[slot], 16)

            def turn(i, k, slot):
                scatter(i, k, slot)
                gather(i + FFN_RING, slot)
                pick_columns(i + FFN_RING, slot)

            for i in range(FFN_RING):
                gather(i, i)
            pool.wait_ge(s_table, 2)
            for i in range(FFN_RING):
                pick_columns(i, i)
            for i in range(FFN_RING):
                turn(i, 0, i)
            with pool.Fori(1, SLOT_TILES // FFN_RING - 1) as k:
                for u in range(FFN_RING):
                    turn(k * FFN_RING + u, k, u)
            used = used_tiles(pool)
            for i in range(SLOT_TILES - FFN_RING, SLOT_TILES):
                with pool.If(used > i):
                    scatter(i, i // FFN_RING, i % FFN_RING)
            turns = SLOT_TILES // FFN_RING
            for slot in range(FFN_RING):
                pool.wait_ge(s_got[slot], 16 * turns)
                pool.wait_ge(s_out[slot], 16 * (turns - 1))
                with pool.If(used > SLOT_TILES - FFN_RING + slot):
                    pool.wait_ge(s_out[slot], 16 * turns)

        @block.scalar
        def _(act):
            def copy_xnT(t, slot, transposed, copied):
                act.wait_ge(transposed, t + 1)
                nc.scalar.activation(xnT[:, slot, :, :, :], p_T[slot][:, :, :, :], ACT.Copy).then_inc(copied, 1)

            def keep_h(t, slot):
                act.wait_ge(s_H, t + 1)
                full = h_full[:, bass.ds(t * CT, CT), :]
                nc.scalar.activation(full, p_agg[slot][:, :, 0:D], ACT.Copy).then_inc(s_hi, 1)
                act.wait_ge(s_hi, 2 * t + 1)
                nc.scalar.activation(h_parts[:, bass.ds(t * CT, CT), 0, :], full, ACT.Copy).then_inc(s_hi, 1)

            copy_xnT(0, 0, s_T, s_Ts)
            with act.Fori(0, (CHUNKS - 1) // 2) as r:
                for u in range(2):
                    copy_xnT(r * 2 + (u + 1), 1 - u, s_T, s_Ts)
                    keep_h(r * 2 + u, u)
            keep_h(CHUNKS - 1, 0)

            def check(c, k, buf, slot):
                if not isinstance(c, int) or c >= 1:
                    act.wait_ge(s_chka, c)
                act.wait_ge(s_adj[buf], 16 * k)
                nc.scalar.activation(junk, adj_bits[buf][:, 0:ACT_PART, 0], ACT.Copy,
                                     accum_out=low_any[:, slot, 0:1]).then_inc(s_chka, 1)

            def low_sum(c, slot):
                act.wait_ge(s_agg, c + 1)
                act.wait_ge(s_free, c + 2)
                nc.scalar.activation(lo_sum[:, :, :], p_agg[slot][:, :, D:2 * D], ACT.Copy).then_inc(s_losum, 1)

            check(0, 1, 0, 0)
            with act.Fori(0, (CHUNKS - 1) // GNN_UNROLL) as r:
                for u in range(GNN_UNROLL):
                    c = r * GNN_UNROLL + (u + 1)
                    check(c, r * 2 + ((u + 1) // ADJ_BUFS + 1), (u + 1) % ADJ_BUFS, (u + 1) % 2)
                    low_sum(c - 1, u % 2)
                    copy_xnT(c - 1, u % 2, s_T2, s_T2s)
            low_sum(CHUNKS - 1, (CHUNKS - 1) % 2)
            copy_xnT(CHUNKS - 1, (CHUNKS - 1) % 2, s_T2, s_T2s)

            act.wait_ge(s_soft, 1)
            nc.scalar.activation(soft, soft, ACT.Exp).then_inc(s_exp, 1)

            HALF = HID // 2

            def relu_hT(i, slot):
                act.wait_ge(s_hT, i + 1)
                if not isinstance(i, int) or i >= 1:
                    act.wait_ge(s_y, i)
                act.wait_ge(s_now, 2 * i + 2)
                for j in range(HB // 2):
                    last = nc.scalar.activation(hT_sb[:, j, :], p_hT[:, j, :], ACT.Relu, bias=b1_now[:, slot, j:j + 1])
                last.then_inc(s_hTa, 1)

            def copy_h(i):
                act.wait_ge(s_h, i + 1)
                if not isinstance(i, int) or i >= 1:
                    act.wait_ge(s_hT, i)
                nc.scalar.activation(h_sb[:, 0:HALF], p_h[:, 0:HALF], ACT.Copy).then_inc(s_hsa, 1)

            def copy_fxT(i):
                act.wait_ge(s_fT, i + 1)
                if not isinstance(i, int) or i >= 1:
                    act.wait_ge(s_h, i)
                nc.scalar.activation(fxT, p_xT, ACT.Copy).then_inc(s_fTs, 1)

            act.wait_ge(s_table, 1)
            copy_fxT(0)
            copy_h(0)
            copy_fxT(1)
            for i in range(FFN_RING):
                relu_hT(i, i)
                copy_h(i + 1)
                copy_fxT(i + 2)
            with act.Fori(1, SLOT_TILES // FFN_RING - 1) as k:
                for u in range(FFN_RING):
                    i = k * FFN_RING + u
                    relu_hT(i, u)
                    copy_h(i + 1)
                    copy_fxT(i + 2)
            used = used_tiles(act)
            for i in range(SLOT_TILES - FFN_RING, SLOT_TILES):
                with act.If(used > i):
                    relu_hT(i, i % FFN_RING)
                    if i + 1 < SLOT_TILES:
                        copy_h(i + 1)
                    if i + 2 < SLOT_TILES:
                        copy_fxT(i + 2)

        @block.tensor
        def _(pe):
            def keep_warm(n, bank):
                for _ in range(n):
                    nc.tensor.matmul(bank[:, 384:512], ones[:, :], ones[:, :], start=True, stop=True)

            pe.wait_ge(s_wsq, 2)
            pe.wait_ge(s_ones, 1)
            for k in range(DK):
                last = nc.tensor.matmul(p_S[:, 0:D], ones[:, :], xn[:, 0, k, :], start=k == 0, stop=k == DK - 1)
            last.then_inc(s_norm, 1)

            def transpose_xn(t, slot, ready, transposed):
                pe.wait_ge(ready, t + 1)
                for j in range(CT):
                    for k in range(DK):
                        last = nc.tensor.transpose(p_T[slot][:, j, k, :], xn[:, slot, j, k * P:(k + 1) * P], ident[:, :])
                last.then_inc(transposed, 1)

            def project(t, slot):
                pe.wait_ge(s_Ts, t + 1)
                if not isinstance(t, int) or t >= 2:
                    pe.wait_ge(s_hi, 2 * t - 3)
                for j in range(CT):
                    for k in range(DK):
                        last = nc.tensor.matmul(p_agg[slot][:, j, 0:D], xnT[:, slot, j, k, :], w_sb[:, k, :],
                                                start=k == 0, stop=k == DK - 1)
                last.then_inc(s_H, 1)

            keep_warm(WARM_START, p_y)
            pe.wait_ge(s_const, 9)
            transpose_xn(0, 0, s_xn, s_T)
            transpose_xn(1, 1, s_xn, s_T)
            keep_warm(WARM_PROJECT, p_y)
            pe.wait_ge(s_wscaled, 1)
            project(0, 0)
            transpose_xn(2, 0, s_xn, s_T)
            project(1, 1)
            with pe.Fori(1, (CHUNKS - 1) // 2) as r:
                for u in range(2):
                    transpose_xn(r * 2 + (u + 1), 1 - u, s_xn, s_T)
                    project(r * 2 + u, u)
            project(CHUNKS - 1, 0)

            pe.wait_ge(s_hi, 2 * CHUNKS - 1)

            def aggregate(c, k_load, buf, slot, k0, k1, j):
                for k in range(k0, k1):
                    nc.tensor.matmul(p_agg[slot][:, j, :], adj_half[buf][:, k, j * P:(j + 1) * P, 1],
                                     h_parts[:, k, :, :], start=k == 0, stop=k == TILES - 1)

            def flags(c, slot):
                pe.wait_ge(s_chka, c + 1)
                pe.wait_ge(s_chkv, c + 1)
                nc.tensor.matmul(p_S[0:1, 0:2], ones[:, 0:1], low_any[:, slot, :], start=True, stop=True).then_inc(s_flag, 1)

            def learn_redo(c):
                pe.wait_ge(s_redo, c + 1)
                pe.nop(nofuse=True)
                return pe.value_load(redo[0:1, 0:1], min_val=0, max_val=1)

            def settle(again, buf, slot):
                with pe.If(again > 0):
                    for j in range(CT):
                        for k in range(TILES):
                            nc.tensor.matmul(p_agg[slot][:, j, 0:D], adj_f32[buf][:, k, j * P:(j + 1) * P],
                                             h_full[:, k, :], start=k == 0, stop=k == TILES - 1, skip_group_check=True)
                        nc.tensor.matmul(p_agg[slot][:, j, D:2 * D], zeros[:, 0:P], zeros[:, :],
                                         start=False, stop=True, skip_group_check=True)
                nc.tensor.matmul(p_S[0:1, 8:9], ones[:, 0:1], ones[:, 0:1], start=True, stop=True).then_inc(s_agg, 1)

            def router(c, slot):
                pe.wait_ge(s_T2s, c + 1)
                for j in range(CT):
                    for k in range(DK):
                        last = nc.tensor.matmul(p_log[slot][:, j, :], xnT[:, slot, j, k, :], wg_sb[:, k, :],
                                                start=k == 0, stop=k == DK - 1)
                last.then_inc(s_log, 1)

            def chunk(c, k_load, buf, slot, before):
                pe.wait_ge(s_adj[buf], 16 * k_load)
                pe.wait_ge(s_free, c + 1)
                if before:
                    aggregate(c, k_load, buf, slot, 0, FLAGS_AT, 0)
                else:
                    for t0, t1 in ((0, CHUNKS - 5), (CHUNKS - 5, CHUNKS - 2), (CHUNKS - 2, CHUNKS)):
                        pe.wait_ge(s_lo, t1)
                        pe.wait_ge(s_hi, 2 * t1)
                        aggregate(c, k_load, buf, slot, t0 * CT, t1 * CT, 0)
                flags(c, slot)
                if before:
                    aggregate(c, k_load, buf, slot, FLAGS_AT, TILES, 0)
                aggregate(c, k_load, buf, slot, 0, TRANSPOSE_AT, 1)
                if before:
                    transpose_xn(c - 1, 1 - slot, s_xn2, s_T2)
                aggregate(c, k_load, buf, slot, TRANSPOSE_AT, ROUTER_AT, 1)
                if before:
                    router(c - 1, 1 - slot)
                again = learn_redo(c)
                aggregate(c, k_load, buf, slot, ROUTER_AT, TILES, 1)
                settle(again, buf, slot)

            chunk(0, 1, 0, 0, False)
            with pe.Fori(0, (CHUNKS - 1) // GNN_UNROLL) as r:
                for u in range(GNN_UNROLL):
                    chunk(r * GNN_UNROLL + (u + 1), r * 2 + ((u + 1) // ADJ_BUFS + 1), (u + 1) % ADJ_BUFS,
                          (u + 1) % 2, True)
            keep_warm(WARM_ROUTER, p_S)
            last_slot = (CHUNKS - 1) % 2
            transpose_xn(CHUNKS - 1, last_slot, s_xn2, s_T2)
            router(CHUNKS - 1, last_slot)
            keep_warm(WARM_RANKS, p_S)

            pe.wait_ge(s_onehot, 1)
            pe.wait_ge(s_T2s, CHUNKS)
            nc.tensor.matmul(p_rank, earlier[:, :], onehot_f, start=True, stop=True).then_inc(s_rank, 1)
            nc.tensor.matmul(p_count, ones[:, :], onehot_f, start=True, stop=True).then_inc(s_rank, 1)
            keep_warm(WARM_TABLE, p_y)
            for k in range(TILES):
                if k == TILES // 2:
                    keep_warm(WARM_TABLE_2, p_y)
                if k * MASK_PARTS % TILES == 0:
                    pe.wait_ge(s_masks, (VALUES + 1) * (k * MASK_PARTS // TILES + 1))
                last = nc.tensor.matmul(p_S[:, 0:VALUES * SLOT_TILES], slot_mask[:, k, :],
                                        tile_mask[:, k, :, :].rearrange("p v i -> p (v i)"),
                                        start=k == 0, stop=k == TILES - 1)
            last.then_inc(s_slots, 1)

            def transpose_fx(i):
                pe.wait_ge(s_fx, i + 1)
                if not isinstance(i, int) or i >= 1:
                    pe.wait_ge(s_fTs, i)
                for k in range(DK):
                    last = nc.tensor.transpose(p_xT[:, k, :], fx[:, k * P:(k + 1) * P], ident[:, :])
                last.then_inc(s_fT, 1)

            def weights_at(i):
                e = pe.value_load(expert_no[0:1, bass.ds(i, 1)], min_val=0, max_val=E - 1)
                pe.wait_ge(s_w[0], 16 * (e // 2) + 16)
                pe.wait_ge(s_w[1], 16 * ((e + 1) // 2) + 16)
                return pe.snap(e * EXPERT_WORDS)

            def hidden(i, at):
                pe.wait_ge(s_fTs, i + 1)
                if not isinstance(i, int) or i >= 1:
                    pe.wait_ge(s_hsa, i)
                    pe.wait_ge(s_hsv, i)
                for n in range(HID // 512):
                    for k in range(DK):
                        last = nc.tensor.matmul(p_h[:, n * 512:(n + 1) * 512], fxT[:, k, :],
                                                arena[:, bass.ds(at + (k * HID + n * 512), 512)],
                                                start=k == 0, stop=k == DK - 1)
                last.then_inc(s_h, 1)

            def transpose_h(i):
                pe.wait_ge(s_hsa, i + 1)
                pe.wait_ge(s_hsv, i + 1)
                if not isinstance(i, int) or i >= 1:
                    pe.wait_ge(s_hTa, i)
                    pe.wait_ge(s_hTv, i)
                for j in range(HB):
                    last = nc.tensor.transpose(p_hT[:, j, :], h_sb[:, j * P:(j + 1) * P], ident[:, :])
                last.then_inc(s_hT, 1)

            def output(i, at, j0, j1):
                if j0 == 0:
                    pe.wait_ge(s_hTa, i + 1)
                    pe.wait_ge(s_hTv, i + 1)
                    if not isinstance(i, int) or i >= 1:
                        pe.wait_ge(s_yb, i)
                for j in range(j0, j1):
                    last = nc.tensor.matmul(p_y[:, 0:D], hT_sb[:, j, :],
                                            arena[:, bass.ds(at + (DK * HID + j * D), D)],
                                            start=j == 0, stop=j == HB - 1)
                if j1 == HB:
                    last.then_inc(s_y, 1)

            keep_warm(WARM_FFN, p_y)
            pe.wait_ge(s_table, 1)
            transpose_fx(0)
            keep_warm(4, p_y)
            hidden(0, weights_at(0))
            transpose_fx(1)

            def tile(i, has1, has2):
                transpose_h(i)
                if has1:
                    hidden(i + 1, weights_at(i + 1))
                at = weights_at(i)
                output(i, at, 0, 6)
                if has2:
                    transpose_fx(i + 2)
                output(i, at, 6, HB)

            for i in range(FFN_RING):
                tile(i, True, True)
            with pe.Fori(1, SLOT_TILES // FFN_RING - 1) as r:
                for u in range(FFN_RING):
                    tile(r * FFN_RING + u, True, True)
            used = used_tiles(pe)
            for i in range(SLOT_TILES - FFN_RING, SLOT_TILES):
                with pe.If(used > i):
                    tile(i, i + 1 < SLOT_TILES, i + 2 < SLOT_TILES)

        @block.vector
        def _(dve):
            chain = Chain(dve, s_dve)
            step = chain.step
            dve.wait_ge(s_wg, 16)
            for k in range(DK):
                nc.vector.tensor_tensor(xn[:, 0, k, :], w_sb[:, k, :], w_sb[:, k, :], ALU.mult).then_inc(s_wsq, 1)
            def row_stats(t, slot):
                for j in range(CT):
                    nc.vector.bn_stats(stats[:, slot, j, :],
                                       x_sb[:, bass.ds(t * CT + j, 1), :].rearrange("p k d -> p (k d)")).then_inc(s_stats, 1)

            def row_means(t, slot):
                dve.wait_ge(s_stats, CT * t + CT)
                dve.nop(nofuse=True)
                for j in range(CT):
                    nc.vector.bn_aggr(mv[:, slot, j, :], stats[:, slot, j, :]).then_inc(s_aggr, 1)

            def row_variances(t, slot):
                dve.wait_ge(s_aggr, CT * t + CT)
                nc.vector.tensor_scalar(rstd[:, slot, :], mv[:, slot, :, 1], EPS, None, ALU.add).then_inc(s_var, 1)

            def row_shifts(t, slot):
                dve.wait_ge(s_rstd, t + 1)
                nc.vector.scalar_tensor_tensor(out=nmr[:, slot, :], in0=mv[:, slot, :, 0], scalar=-1.0,
                                               in1=rstd[:, slot, :], op0=ALU.mult, op1=ALU.mult).then_inc(s_nmr, 1)

            def normalize(t, slot):
                dve.wait_ge(s_nmr, t + 1)
                if not isinstance(t, int) or t >= 2:
                    dve.wait_ge(s_T, t - 1)
                elif t == 0:
                    dve.wait_ge(s_norm, 1)
                for j in range(CT):
                    last = nc.vector.tensor_scalar(xn[:, slot % 2, j, :], x_sb[:, bass.ds(t * CT + j, 1), :].rearrange("p k d -> p (k d)"),
                                                   rstd[:, slot, j:j + 1], nmr[:, slot, j:j + 1], ALU.mult, ALU.add)
                last.then_inc(s_xn, 1)

            def turn(t, slot):
                follow = CHUNKS - 1 - t if isinstance(t, int) else CHUNKS
                if follow >= 2:
                    normalize(t + 2, (slot + 2) % AHEAD)
                if follow >= AHEAD:
                    row_stats(t + AHEAD, slot)
                    row_means(t + AHEAD, slot)
                if follow >= AHEAD:
                    row_variances(t + AHEAD, slot)
                if follow >= 3:
                    row_shifts(t + 3, (slot + 3) % AHEAD)

            def scale_w():
                bits = lo_sum[:, 0, :].bitcast(I32)
                scale = lo_sum[:, 1, :]
                inv_bits = inv_scale[:, :].bitcast(I32)
                dve.wait_ge(s_norm, 1)
                step(nc.vector.tensor_scalar(lo_sum[:, 0, :], p_S[:, 0:D], 2.0, None, ALU.mult))
                step(nc.vector.tensor_scalar(bits, bits, 24, None, ALU.logical_shift_right))
                step(nc.vector.tensor_scalar(scale.bitcast(I32), bits, -float(1 << 23), float(SCALE_EXP << 23), ALU.mult, ALU.add))
                step(nc.vector.tensor_scalar(inv_bits, bits, float(1 << 23), float(INV_EXP << 23), ALU.mult, ALU.add))
                nc.vector.tensor_tensor(w_sb[:, :, :], w_sb[:, :, :], scale.unsqueeze(1).to_broadcast([P, DK, D]),
                                        ALU.mult).then_inc(s_wscaled, 1)

            dve.wait_ge(s_x[0], 16)
            row_stats(0, 0)
            row_means(0, 0)
            row_variances(0, 0)
            row_stats(1, 1)
            row_means(1, 1)
            row_variances(1, 1)
            row_shifts(0, 0)
            normalize(0, 0)
            row_stats(2, 2)
            row_shifts(1, 1)
            normalize(1, 1)
            row_means(2, 2)
            row_variances(2, 2)
            scale_w()
            row_shifts(2, 2)
            row_stats(3, 3)
            row_means(3, 3)
            row_variances(3, 3)
            dve.wait_ge(s_x[1], 16)
            turn(0, 0)
            with dve.Fori(0, (CHUNKS - 1 - AHEAD) // AHEAD) as r:
                for u in range(AHEAD):
                    turn(r * AHEAD + (u + 1), (u + 1) % AHEAD)
            for t in range(CHUNKS - AHEAD, CHUNKS):
                turn(t, t % AHEAD)

            dve.wait_ge(s_const, 9)
            step(nc.vector.memset(scan_ones[:, :], 1.0))
            step(nc.vector.tensor_scalar(is_token[:, :], padding[:, :], -1.0, 1.0, ALU.mult, ALU.add))

            def check(c, k_load, buf, slot):
                dve.wait_ge(s_adj[buf], 16 * k_load)
                nc.vector.tensor_reduce(low_any[:, slot, 1:2], adj_bits[buf][:, ACT_PART:CHUNK_WORDS, 0],
                                        AX.X, ALU.max).then_inc(s_chkv, 1)

            def decide(c):
                dve.wait_ge(s_flag, c + 1)
                nc.vector.tensor_reduce(low_top[:, :], p_S[0:1, 0:2], AX.X, ALU.max).then_inc(s_lowtop, 1)
                dve.wait_ge(s_lowtop, c + 1)
                nc.vector.tensor_scalar(redo[:, :], low_top[:, :], 0.0, None, ALU.is_gt).then_inc(s_redo, 1)

            STEPS = 2 + 2 * CT
            finish_base = chain.n

            def finish(c, slot):
                chain.enter(c * STEPS + finish_base)
                r = rows[:, slot, :, 0:D]
                dve.wait_ge(s_losum, c + 1)
                dve.wait_ge(s_rowfree, c + 1)
                nc.vector.tensor_tensor(r, p_agg[slot][:, :, 0:D], lo_sum[:, :, :], ALU.add).then_inc(s_free, 1)
                dve.wait_ge(s_free, c + 3)
                step(nc.vector.tensor_tensor(r, r, inv_scale[:, :].unsqueeze(1).to_broadcast([P, CT, D]), ALU.mult))
                dve.wait_ge(s_xb, CT * c + CT)
                step(nc.vector.tensor_tensor(r, r, x_sb[:, bass.ds(c * CT, CT), :], ALU.add))
                for j in range(CT):
                    chain.mark(nc.vector.bn_stats(stats2[:, j, :], rows[:, slot, j, 0:D]))
                chain.wait()
                dve.nop(nofuse=True)
                for j in range(CT):
                    chain.mark(nc.vector.bn_aggr(mv2[:, j, :], stats2[:, j, :]))
                chain.wait()
                nc.vector.tensor_scalar(mv2[:, :, 1], mv2[:, :, 1], EPS, None, ALU.add).then_inc(s_var2, 1)
                dve.wait_ge(s_rstd2, c + 1)
                nc.vector.scalar_tensor_tensor(out=rows[:, slot, :, D + 1], in0=mv2[:, :, 0], scalar=-1.0,
                                               in1=rows[:, slot, :, D], op0=ALU.mult, op1=ALU.mult).then_inc(s_row, 1)
                dve.wait_ge(s_row, c + 1)
                for j in range(CT):
                    last = nc.vector.tensor_scalar(xn[:, slot, j, :], rows[:, slot, j, 0:D], rows[:, slot, j, D:D + 1],
                                                   rows[:, slot, j, D + 1:D + 2], ALU.mult, ALU.add)
                last.then_inc(s_xn2, 1)

            def keep_logits(c, slot):
                dve.wait_ge(s_log, c + 1)
                nc.vector.tensor_tensor(logits[:, bass.ds(c * CT, CT), :], p_log[slot], bg_sb[:, :, :],
                                        ALU.add).then_inc(s_logs, 1)

            dve.sem_inc(s_free, 2)
            dve.wait_ge(s_small, SMALL)
            check(0, 1, 0, 0)
            decide(0)
            with dve.Fori(0, (CHUNKS - 1) // GNN_UNROLL) as r:
                for u in range(GNN_UNROLL):
                    c = r * GNN_UNROLL + (u + 1)
                    check(c, r * 2 + ((u + 1) // ADJ_BUFS + 1), (u + 1) % ADJ_BUFS, (u + 1) % 2)
                    decide(c)
                    finish(c - 1, u % 2)
                    keep_logits(c - 1, u % 2)
            finish(CHUNKS - 1, (CHUNKS - 1) % 2)
            keep_logits(CHUNKS - 1, (CHUNKS - 1) % 2)
            chain.enter(finish_base + CHUNKS * STEPS)
            dve.wait_ge(s_logs, CHUNKS)

            def over_experts(a):
                return a.unsqueeze(2).to_broadcast([P, TILES, E])

            step(nc.vector.tensor_reduce(top, logits[:, :, :], AX.X, ALU.max))
            nc.vector.tensor_tensor(soft, logits[:, :, :], over_experts(top), ALU.subtract).then_inc(s_soft, 1)
            step(nc.vector.tensor_tensor(pick, logits[:, :, :], over_experts(top), ALU.is_equal))
            step(nc.vector.tensor_tensor(pick, pick, down[:, :].unsqueeze(1).to_broadcast([P, TILES, E]), ALU.mult))
            step(nc.vector.tensor_reduce(first, pick, AX.X, ALU.max))
            step(nc.vector.tensor_tensor(pick, pick, over_experts(first), ALU.is_equal))
            nc.vector.tensor_tensor(onehot, pick.rearrange("p k e -> p e k"),
                                    is_token[:, :].unsqueeze(1).to_broadcast([P, E, TILES]), ALU.mult).then_inc(s_onehot, 1)
            step(nc.vector.memset(running[:, 0:1], 0.0))
            dve.wait_ge(s_exp, 1)
            step(nc.vector.tensor_reduce(score, soft, AX.X, ALU.add))
            step(nc.vector.reciprocal(score, score))
            step(nc.vector.tensor_copy(values[:, :, 2], score))
            step(nc.vector.tensor_tensor(rest, score, values[:, :, 2], ALU.subtract))
            step(nc.vector.tensor_copy(values[:, :, 3], rest))
            step(nc.vector.tensor_tensor(values[:, :, 4], rest, values[:, :, 3], ALU.subtract))
            dve.wait_ge(s_rank, 2)
            step(nc.vector.tensor_tensor_scan(running[:, 1:1 + E * TILES], scan_ones[:, :], p_count, 0.0, ALU.mult, ALU.add))
            run_start = running[:, 0:E * TILES].rearrange("p (e k) -> p e k", e=E)
            run_end = running[:, 1:1 + E * TILES].rearrange("p (e k) -> p e k", e=E)
            step(nc.vector.tensor_tensor(tiles_f, run_end[:, :, TILES - 1], run_start[:, :, 0], ALU.subtract))
            step(nc.vector.tensor_scalar(tiles_i, tiles_f, float(P - 1), None, ALU.add))
            step(nc.vector.tensor_scalar(tiles_i, tiles_i, P.bit_length() - 1, None, ALU.logical_shift_right))
            step(nc.vector.tensor_copy(tiles_f, tiles_i))
            step(nc.vector.tensor_tensor_scan(tile_end, scan_ones[:, 0:E], tiles_f, 0.0, ALU.mult, ALU.add))
            step(nc.vector.tensor_tensor(start_e, tile_end, tiles_f, ALU.subtract))
            step(nc.vector.scalar_tensor_tensor(out=start_e, in0=start_e, scalar=float(P), in1=run_start[:, :, 0],
                                                op0=ALU.mult, op1=ALU.subtract))
            step(nc.vector.tensor_tensor(slot_no, run_start, start_e.unsqueeze(2).to_broadcast([P, E, TILES]), ALU.add))
            step(nc.vector.tensor_tensor(slot_no, slot_no, p_rank.rearrange("p (e k) -> p e k", e=E), ALU.add))
            step(nc.vector.tensor_tensor(slot_no, slot_no, onehot, ALU.mult))
            step(nc.vector.tensor_reduce(pos, slot_no.rearrange("p e k -> p k e"), AX.X, ALU.add))
            step(nc.vector.scalar_tensor_tensor(out=pos, in0=padding[:, :], scalar=float(SLOT_TILES * P), in1=pos,
                                                op0=ALU.mult, op1=ALU.add))
            step(nc.vector.tensor_copy(pos_i[:, 2, :], pos))
            step(nc.vector.tensor_scalar(pos_i[:, 0, :], pos_i[:, 2, :], P.bit_length() - 1, None, ALU.logical_shift_right))
            step(nc.vector.tensor_scalar(pos_i[:, 1, :], pos_i[:, 2, :], P - 1, None, ALU.bitwise_and))
            step(nc.vector.tensor_copy(pos_b, pos_i[:, 0:2, :]))
            for part in range(MASK_PARTS):
                k0, k1 = part * TILES // MASK_PARTS, (part + 1) * TILES // MASK_PARTS
                n = k1 - k0
                step(nc.vector.tensor_tensor(in_tile[:, k0:k1, :], iota_tile_b[:, :].unsqueeze(1).to_broadcast([P, n, SLOT_TILES]),
                                             pos_b[:, 0, k0:k1].unsqueeze(2).to_broadcast([P, n, SLOT_TILES]), ALU.is_equal))
                for v in range(VALUES):
                    nc.vector.tensor_tensor(tile_mask[:, k0:k1, v, :], in_tile[:, k0:k1, :],
                                            values[:, k0:k1, v].unsqueeze(2).to_broadcast([P, n, SLOT_TILES]),
                                            ALU.mult).then_inc(s_masks, 1)
                nc.vector.tensor_tensor(slot_mask[:, k0:k1, :], iota_slot_b[:, :].unsqueeze(1).to_broadcast([P, n, P]),
                                        pos_b[:, 1, k0:k1].unsqueeze(2).to_broadcast([P, n, P]), ALU.is_equal).then_inc(s_masks, 1)
            step(nc.vector.tensor_tensor(ended, iota_tile[0:1, :].unsqueeze(2).to_broadcast([1, SLOT_TILES, E]),
                                         tile_end[0:1, :].unsqueeze(1).to_broadcast([1, SLOT_TILES, E]), ALU.is_ge))
            step(nc.vector.tensor_reduce(expert_f, ended, AX.X, ALU.add))
            step(nc.vector.tensor_scalar(expert_no[:, :], expert_f, float(E - 1), None, ALU.min))
            step(nc.vector.tensor_copy(tiles_used[:, :], tile_end[0:1, E - 1:E]))
            dve.wait_ge(s_slots, 1)
            step(nc.vector.tensor_copy(table, p_S[:, 0:VALUES * SLOT_TILES]))
            step(nc.vector.tensor_scalar(row_f, table[:, 1, :], 1.0, SKIP, ALU.is_lt, ALU.mult))
            step(nc.vector.scalar_tensor_tensor(out=row_f, in0=table[:, 1, :], scalar=-1.0, in1=row_f,
                                                op0=ALU.add, op1=ALU.add))
            nc.vector.scalar_tensor_tensor(out=slot_row[:, :], in0=table[:, 0, :], scalar=float(P), in1=row_f,
                                           op0=ALU.mult, op1=ALU.add).then_inc(s_table, 1)
            step(nc.vector.tensor_tensor(slot_score[:, :], table[:, 2, :], table[:, 3, :], ALU.add))
            nc.vector.tensor_tensor(slot_score[:, :], slot_score[:, :], table[:, 4, :], ALU.add).then_inc(s_table, 1)
            dve.wait_ge(s_table, 2)
            dve.wait_ge(s_w[1], 16)

            HALF = HID // 2

            def relu_hT(i, slot):
                dve.wait_ge(s_hT, i + 1)
                if not isinstance(i, int) or i >= 1:
                    dve.wait_ge(s_y, i)
                dve.wait_ge(s_now, 2 * i + 2)
                for j in range(HB // 2, HB):
                    last = nc.vector.tensor_scalar(hT_sb[:, j, :], p_hT[:, j, :], b1_now[:, slot, j:j + 1], 0.0,
                                                   ALU.add, ALU.max)
                last.then_inc(s_hTv, 1)

            def copy_h(i):
                dve.wait_ge(s_h, i + 1)
                if not isinstance(i, int) or i >= 1:
                    dve.wait_ge(s_hT, i)
                nc.vector.tensor_copy(h_sb[:, HALF:HID], p_h[:, HALF:HID]).then_inc(s_hsv, 1)

            def normalize_rows(i, k, slot):
                dve.wait_ge(s_got[slot], 16 * k + 16)
                if not isinstance(i, int) or i >= 1:
                    dve.wait_ge(s_fT, i)
                g = got[slot]
                nc.vector.tensor_scalar(fx, g[:, 0:D], g[:, D:D + 1], g[:, D + 1:D + 2], ALU.mult, ALU.add).then_inc(s_fx, 1)

            def finish_rows(i, k, slot):
                e = dve.value_load(expert_no[0:1, bass.ds(i, 1)], min_val=0, max_val=E - 1)
                dve.wait_ge(s_y, i + 1)
                nc.vector.tensor_tensor(yb, p_y[:, 0:D], b2_sb[:, bass.ds(e, 1), :].rearrange("p e d -> p (e d)"),
                                        ALU.add).then_inc(s_yb, 1)
                dve.wait_ge(s_yb, i + 1)
                if not isinstance(k, int) or k >= 1:
                    dve.wait_ge(s_out[slot], 16 * k)
                nc.vector.scalar_tensor_tensor(out=done[slot], in0=yb, scalar=score_now[:, slot:slot + 1],
                                               in1=got[slot][:, 0:D], op0=ALU.mult, op1=ALU.add).then_inc(s_done, 1)

            normalize_rows(0, 0, 0)
            normalize_rows(1, 0, 1)
            copy_h(0)
            for i in range(FFN_RING):
                relu_hT(i, i)
                copy_h(i + 1)
                normalize_rows(i + 2, (i + 2) // FFN_RING, (i + 2) % FFN_RING)
                finish_rows(i, 0, i)
            with dve.Fori(1, SLOT_TILES // FFN_RING - 1) as k:
                for u in range(FFN_RING):
                    i = k * FFN_RING + u
                    relu_hT(i, u)
                    copy_h(i + 1)
                    normalize_rows(i + 2, k + (u + 2) // FFN_RING, (u + 2) % FFN_RING)
                    finish_rows(i, k, u)
            used = used_tiles(dve)
            for i in range(SLOT_TILES - FFN_RING, SLOT_TILES):
                with dve.If(used > i):
                    relu_hT(i, i % FFN_RING)
                    if i + 1 < SLOT_TILES:
                        copy_h(i + 1)
                    if i + 2 < SLOT_TILES:
                        normalize_rows(i + 2, (i + 2) // FFN_RING, (i + 2) % FFN_RING)
                    finish_rows(i, i // FFN_RING, i % FFN_RING)


def kernel(x, adj, L0_gnn_W, L0_gnn_b, L0_ffn_Wg, L0_ffn_bg, L0_ffn_W1, L0_ffn_b1, L0_ffn_W2, L0_ffn_b2):
    import numpy as np
    import concourse.bacc as bacc
    from concourse.bass_utils import run_bass_kernel_spmd

    x, adj = np.asarray(x), np.asarray(adj)
    x_pad = np.zeros((NPAD, D), x.dtype)
    x_pad[:N] = x
    adj_t = np.zeros((NPAD, NPAD), adj.dtype)
    adj_t[:N, :N] = adj.T
    w1, w2 = np.asarray(L0_ffn_W1), np.asarray(L0_ffn_W2)
    arrays = {
        "x": x_pad.reshape(TILES, P, D).transpose(1, 0, 2),
        "adj": adj_t.reshape(TILES, P, CHUNKS, CT * P).transpose(2, 1, 0, 3).reshape(CHUNKS, P, CHUNK_WORDS),
        "w_gnn": np.asarray(L0_gnn_W).transpose(1, 0, 2).reshape(DK, P, D).transpose(1, 0, 2),
        "b_gnn": np.asarray(L0_gnn_b).reshape(1, D),
        "w_gate": np.asarray(L0_ffn_Wg).reshape(DK, P, E).transpose(1, 0, 2),
        "b_gate": np.asarray(L0_ffn_bg).reshape(1, E),
        "w_exp": np.concatenate([w1.reshape(E, DK, P, HID).transpose(0, 2, 1, 3).reshape(E, P, DK * HID),
                                 w2.reshape(E, HB, P, D).transpose(0, 2, 1, 3).reshape(E, P, HB * D)], axis=2),
        "b1": np.asarray(L0_ffn_b1).reshape(E, HB, P).transpose(2, 0, 1),
        "b2": np.asarray(L0_ffn_b2).reshape(1, E * D),
    }
    arrays = {name: np.ascontiguousarray(a) for name, a in arrays.items()}
    nc = bacc.Bacc("TRN2", target_bir_lowering=False, num_devices=1)
    args = [nc.dram_tensor(name, a.shape, mybir.dt.from_np(a.dtype), kind="ExternalInput").ap()
            for name, a in arrays.items()]
    out = nc.dram_tensor("out", (N, D), F32, kind="ExternalOutput").ap()
    build(nc, *args, out)
    r = run_bass_kernel_spmd(nc, [arrays], core_ids=[0])
    return r.results[0]["out"]
```
